# Optimizing a Trainium2 kernel written in Bass

```python
import numpy as np
import jax
import jax.numpy as jnp

def _softmax(x, axis=-1):
    return jax.nn.softmax(x, axis=axis)

def _gelu(x):
    return jax.nn.gelu(x, approximate=True)

def _silu(x):
    return jax.nn.silu(x)

def _sigmoid(x):
    return jax.nn.sigmoid(x)

def _layernorm(x, axis=-1, eps=1e-05):
    m = jnp.mean(x, axis=axis, keepdims=True)
    v = jnp.var(x, axis=axis, keepdims=True)
    return (x - m) / jnp.sqrt(v + eps)

def _scatter_add(tgt, idx, src, axis=0):
    return tgt.at[idx].add(src)

def _segment_sum(src, seg, n):
    return jax.ops.segment_sum(src, seg, n)
kernel_name = 'mk_adj_resnorm_d2_adj_r2_0b3b0b'

def setup_inputs(seed: int=0):
    np.random.seed(seed)
    _w = jnp.asarray

    def _rec_inputs():
        import jax
        import jax.numpy as jnp
        _gk = jax.random.key(seed)
        x = -0.0005207 + 1.001 * jax.random.normal(jax.random.fold_in(_gk, 1), (4096, 128), jnp.float32)
        _w = (1.0 + jnp.arange(4096, dtype=jnp.float32)) ** (-0.5)
        _w = _w / _w.mean()
        _pij = jnp.clip(0.000976562 * _w[:, None] * _w[None, :], 0.0, 1.0)
        _a = jax.random.uniform(jax.random.fold_in(_gk, 2), (4096, 4096)) < _pij
        _a = jnp.logical_or(_a, jnp.eye(4096, dtype=bool))
        _af = _a.astype(jnp.float32)
        _af = _af * jax.random.uniform(jax.random.fold_in(_gk, 3), (4096, 4096), jnp.float32, 0.05, 1)
        adj = _af
        return (x, adj)
    x, adj = _rec_inputs()

    def _L0_gnn_setup():
        import jax, jax.numpy as jnp
        import numpy as np
        N, F_IN, F_OUT = (4096, 128, 128)
        key = jax.random.key(seed)
        k1, k2, k3, k4 = jax.random.split(key, 4)
        X = jax.random.normal(k1, (N, F_IN), dtype=jnp.float32)
        A = jax.random.uniform(k2, (N, N), dtype=jnp.float32)
        W = jax.random.normal(k3, (F_OUT, F_IN), dtype=jnp.float32) * (1.0 / np.sqrt(F_IN))
        b = jax.random.normal(k4, (F_OUT,), dtype=jnp.float32) * 0.01
        return {'X': X, 'A': A, 'W': W, 'b': b}
    _L0_gnn_all = _L0_gnn_setup()
    _L0_gnn_in = {k: v for k, v in _L0_gnn_all.items() if k in ('W', 'b')}
    del _L0_gnn_all

    def _L1_gnn_setup():
        import jax, jax.numpy as jnp
        import numpy as np
        N = 4096
        F_IN = 128
        F_OUT = 128
        key = jax.random.key(seed)
        k_x, k_adj, k_kernel, k_bias, k_beta = jax.random.split(key, 5)
        x = jax.random.normal(k_x, (N, F_IN), dtype=jnp.float32)
        adj = jax.random.uniform(k_adj, (N, N), dtype=jnp.float32)
        limit = float(np.sqrt(6.0 / (F_IN + F_OUT)))
        kernel = jax.random.uniform(k_kernel, (F_IN, F_OUT), dtype=jnp.float32, minval=-limit, maxval=limit)
        bias = 0.01 * jax.random.normal(k_bias, (F_OUT,), dtype=jnp.float32)
        beta = 0.01 * jax.random.normal(k_beta, (N,), dtype=jnp.float32)
        return {'x': x, 'adj': adj, 'kernel': kernel, 'bias': bias, 'beta': beta}
    _L1_gnn_all = _L1_gnn_setup()
    _L1_gnn_in = {k: v for k, v in _L1_gnn_all.items() if k in ('kernel', 'bias', 'beta')}
    del _L1_gnn_all
    return {'x': x, 'adj': adj, 'L0_gnn_W': _L0_gnn_in['W'], 'L0_gnn_b': _L0_gnn_in['b'], 'L1_gnn_kernel': _L1_gnn_in['kernel'], 'L1_gnn_bias': _L1_gnn_in['bias'], 'L1_gnn_beta': _L1_gnn_in['beta']}

def reference(x, adj, L0_gnn_W, L0_gnn_b, L1_gnn_kernel, L1_gnn_bias, L1_gnn_beta):
    import jax
    import jax.numpy as jnp

    def _L0_gnn_ref(X, A, W, b):
        import jax, jax.numpy as jnp
        import numpy as np
        N, F_IN, F_OUT = (4096, 128, 128)
        A_hat = A + jnp.eye(A.shape[0], dtype=A.dtype)
        deg = jnp.sum(A_hat, axis=1)
        d = jnp.where(deg > 0, jax.lax.rsqrt(deg), 0.0)
        A_norm = d[:, None] * A_hat * d[None, :]
        out = A_norm @ X
        out = out @ W.T + b
        return out

    def _L1_gnn_ref(x, adj, kernel, bias, beta):
        import jax, jax.numpy as jnp
        import numpy as np
        N = 4096
        F_IN = 128
        F_OUT = 128
        scale = jnp.reciprocal(jnp.sum(adj, axis=1) + beta)
        agg = adj @ x + beta[:, None] * x
        return scale[:, None] * agg @ kernel + bias
    x = _layernorm(x + _L0_gnn_ref(x, adj, L0_gnn_W, L0_gnn_b), axis=-1)
    x = _layernorm(x + _L1_gnn_ref(x, adj, L1_gnn_kernel, L1_gnn_bias, L1_gnn_beta), axis=-1)
    return x

_drawn_inputs = setup_inputs


def setup_inputs(seed=0):
    import zlib

    import numpy as np

    out = dict(_drawn_inputs(seed))
    spreads = {}
    factors = {'L0_gnn_b': 5.583, 'L1_gnn_bias': 7.002, 'L1_gnn_beta': 8.0}
    for name, (base, spread) in spreads.items():
        noise = np.random.default_rng([zlib.crc32(name.encode()), seed]).standard_normal(out[name].shape)
        drawn = base * np.exp(spread * noise) if base else spread * noise
        out[name] = jnp.asarray(drawn.astype(out[name].dtype))
    for name, factor in factors.items():
        out[name] = (out[name] * factor).astype(out[name].dtype)
    return out
```

```python
from contextlib import ExitStack

import concourse.bass as bass
from concourse import mybir

N = 4096
F = 128
P = 128
NP = 8
B = N // NP
T = B // P
HALF = T // 2 * B
SLOTS = 13
KEEP = 3
NATIVE = [0, 1, 2, 3, 4, 7]
NHI, NLO = 4, 2
EPS = 1e-5
TINY = 1.2e-38
LAST = NP - 1
FINAL = [4, 5, 6, 0, 1, 2, 3]
STORES = 2


class Use:

    def __init__(self, J, I):
        self.J, self.I, self.native = J, I, J in NATIVE


class Load:

    def __init__(self, J, I, degree_pos):
        self.J, self.I, self.degree_pos = J, I, degree_pos
        self.waits = {}


def layer0_uses():
    stages = []
    for t in range(NP):
        row = [Use(t - 1, I) for I in range(t - 1, -1, -1)]
        column = [Use(J, t) for J in range(t)]
        if t == LAST:
            held, column = column[:t - 2], column[t - 2:]
        cut = max(len(column) - 2, 0) if t < LAST else 0
        stages.append((row + column[:cut], column[cut:]))
    final = [Use(LAST, I) for I in FINAL]
    closing = held + [Use(LAST, LAST)]
    return stages, final, closing


def layer0_loads():
    stages = []
    for t in range(NP):
        loads = [Load(J, t, J - t) for J in range(t, NP)]
        loads += [Load(t - 1, I, None) for I in range(t - 2 - KEEP, -1, -1)]
        loads += [Load(J, t, NP - t + J) for J in range(t)]
        stages.append(loads)
    again = [Load(LAST, I, None) for I in FINAL if LAST - I > KEEP]
    return stages, again


def degree_count(t, pos):
    return (NP - 1) * t + max(pos, 1)


def place_blocks():
    use_stages, final, closing = layer0_uses()
    load_stages, again = layer0_loads()
    uses = [u for pre, post in use_stages for u in pre + post] + final + closing
    loads = [l for st in load_stages for l in st] + again
    native = split = 0
    for u in uses:
        if u.native:
            u.index, native = native, native + 1
        else:
            u.index, split = split, split + 1
    first_layer = split
    reuse = [Use(J, LAST) for J in range(NP)]
    for J, u in enumerate(reuse):
        u.native, u.index = False, first_layer + J
    next_panel = [Load(J, LAST - 1, None) for J in range(NP)]
    free = [(s, {}) for s in range(SLOTS)]
    held = {}
    queue = list(uses) + reuse
    dropped = []
    taken = {s: 0 for s in range(SLOTS)}
    position = 0
    for n, l in enumerate(loads + next_panel):
        while not free:
            if dropped:
                d = dropped.pop(0)
                free.append((d.slot, {"degrees": degree_count(d.I, d.degree_pos)}))
                continue
            u = queue[position]
            b = held[(u.J, u.I)]
            u.load = b
            position += 1
            if u.I == LAST and u in uses:
                continue
            waits = {"native": u.index + 1} if u.native else {"split": 2 * u.index + 2}
            if b.degree_pos is not None:
                waits["degrees"] = degree_count(b.I, b.degree_pos)
            free.append((b.slot, waits))
            del held[(u.J, u.I)]
        l.slot, l.waits = free.pop(0)
        l.number, l.position = n, position
        taken[l.slot] += 1
        l.arrived = 16 * taken[l.slot]
        if l.degree_pos is not None and l.J - l.I > KEEP:
            dropped.append(l)
            if l.I == LAST:
                raise AssertionError
        else:
            held[(l.J, l.I)] = l
    for u in queue[position:]:
        u.load = held[(u.J, u.I)]
    for n, u in enumerate(queue):
        u.position = n
    return use_stages, final, closing, load_stages, again, reuse, next_panel, native, first_layer, taken


def two_gnn_layers(nc, x, adj, w0t, b0, w1, b1, beta, out):
    f32, f32r = mybir.dt.float32, mybir.dt.float32r
    ALU, ACT = mybir.AluOpType, mybir.ActivationFunctionType
    use_stages, final, closing, load_stages, again, reuse, next_panel, natives, splits0, taken = place_blocks()
    ring = [l.slot for l in next_panel]
    arrived1 = [l.arrived for l in next_panel]

    ctx = ExitStack()
    with ctx:
        def sb(name, shape, dt=f32):
            return ctx.enter_context(nc.sbuf_tensor(name, shape, dt))

        def sem(name):
            return ctx.enter_context(nc.semaphore(name))

        blocks = sb("blocks", [P, SLOTS, T * B])
        feat = sb("feat", [P, NP, T * F])
        hi_f = sb("hi_f", [P, NP, T * F], f32r)
        lo_f = sb("lo_f", [P, NP, T * F], f32r)
        scaled = sb("scaled", [P, len(NATIVE), T * F])
        hi_a = sb("hi_a", [P, NHI, HALF], f32r)
        lo_a = sb("lo_a", [P, NLO, HALF], f32r)
        work = sb("work", [P, T * B])
        part = work[:, :]
        z = work[:, 0:2 * B].rearrange("p (s c) -> p s c", s=2)
        agg = work[:, 2 * B:4 * B].rearrange("p (s c) -> p s c", s=2)
        w0_sb, w1_sb = sb("w0_sb", [F, F]), sb("w1_sb", [F, F])
        b0_sb, b1_sb = sb("b0_sb", [P, T * F]), sb("b1_sb", [P, T * F])
        ident, ident_r = sb("ident", [P, P]), sb("ident_r", [P, P], f32r)
        self_f = sb("self_f", [P, T * F])
        biased = sb("biased", [P, T * F])
        ones = sb("ones", [P, 1])
        neg_half = sb("neg_half", [P, T])
        beta_sb, rowsum = sb("beta_sb", [P, NP * T]), sb("rowsum", [P, NP * T])
        dinv = sb("dinv", [P, NP * T])
        scale = sb("scale", [P, NP * T])
        positive, clamped, power = sb("positive", [P, T]), sb("clamped", [P, T]), sb("power", [P, T])
        scale4, beta4 = sb("scale4", [P, T]), sb("beta4", [P, T])
        stats, meanvar = sb("stats", [P, T, 6]), sb("meanvar", [P, T, 2])
        eps = sb("eps", [P, T])
        vareps, rstd = sb("vareps", [P, T]), sb("rstd", [P, T])

        bank = [ctx.enter_context(nc.psum_tensor(f"bank{i}", [P, B], f32)) for i in range(NP)]

        block_in = [sem(f"block_in{s}") for s in range(SLOTS)]
        x_in = [sem(f"x_in{t}") for t in range(NP)]
        consts_in = sem("consts_in")
        ident_zero, consts_set, ident_done, ident_r_done = (sem(n) for n in ("ident_zero", "consts_set", "ident_done", "ident_r_done"))
        degrees = sem("degrees")
        rowsum_ready = sem("rowsum_ready")
        rowsum_saved = sem("rowsum_saved")
        pool_step, vec_step, act_step = sem("pool_step"), sem("vec_step"), sem("act_step")
        dinv_ready = sem("dinv_ready")
        y_ready = sem("y_ready")
        hi_ready, lo_ready = sem("hi_ready"), sem("lo_ready")
        half_used = sem("half_used")
        native_used = sem("native_used")
        agg_ready = sem("agg_ready")
        proj_ready, proj_read = sem("proj_ready"), sem("proj_read")
        var_ready, rstd_ready = sem("var_ready"), sem("rstd_ready")
        x1_ready = sem("x1_ready")
        self_ready = sem("self_ready")
        biased_ready = sem("biased_ready")
        scale_set = sem("scale_set")
        rows_ready = sem("rows_ready")
        stored = [sem(f"stored{i}") for i in range(STORES)]

        x_v = x.rearrange("(b p k) f -> b p (k f)", b=NP, p=P)
        out_v = out.rearrange("(b p k) f -> b p (k f)", b=NP, p=P)
        adj_flat = adj.rearrange("i j p c -> (i j p c)")
        x1_order = FINAL + [LAST]

        def split_of(s, J):
            return splits0 + NP * s + J

        def columns(s):
            if isinstance(s, int):
                return slice(s * T, (s + 1) * T)
            return bass.ds(s * T, T)

        def arrival(s, J):
            if isinstance(s, int) and s == 0:
                return reuse[J].load.slot, reuse[J].load.arrived
            return ring[J], arrived1[J] + (s - 1) * 16

        block = ctx.enter_context(nc.Block())

        @block.sync
        def _(sync):
            def load(l):
                if "degrees" in l.waits:
                    sync.wait_ge(degrees, l.waits["degrees"])
                if "native" in l.waits:
                    sync.wait_ge(native_used, l.waits["native"])
                if "split" in l.waits:
                    sync.wait_ge(lo_ready, l.waits["split"])
                sync.dma_start(blocks[:, l.slot, :], adj[LAST - l.I, LAST - l.J, :, :]).then_inc(block_in[l.slot], 16)

            for t in range(NP):
                for n, l in enumerate(load_stages[t]):
                    load(l)
                    if n == NP - 3:
                        sync.dma_start(feat[:, LAST - t, :], x_v[LAST - t, :, :]).then_inc(x_in[t], 16)
            for l in again + next_panel:
                load(l)
            with sync.Fori(0, NP // 2 - 1) as r:
                for u in range(2):
                    s = 2 * r + (2 + u)
                    for J in range(NP):
                        start = sync.snap((s * NP + (LAST - J)) * (P * T * B))
                        source = adj_flat[bass.ds(start, P * T * B)].rearrange("(p c) -> p c", p=P)
                        sync.wait_ge(lo_ready, 2 * split_of(s - 1, J) + 2)
                        sync.dma_start(blocks[:, ring[J], :], source).then_inc(block_in[ring[J]], 16)

        @block.gpsimd
        def _(pool):
            nc.gpsimd.memset(ident[:, :], 0.0).then_inc(ident_zero, 1)
            nc.gpsimd.memset(ones[:, :], 1.0).then_inc(consts_set, 1)
            nc.gpsimd.memset(neg_half[:, :], -0.5).then_inc(consts_set, 1)
            nc.gpsimd.memset(eps[:, :], EPS).then_inc(consts_set, 1)
            pool.wait_ge(ident_zero, 1)
            nc.gpsimd.affine_select(out=ident[:, :], in_=ident[:, :], compare_op=ALU.not_equal, fill=1.0,
                                    base=0, pattern=[[-1, P]], channel_multiplier=1).then_inc(ident_done, 1)
            pool.wait_ge(consts_set, 3)
            for t in range(NP):
                pool.wait_ge(rowsum_saved, t + 1)
                cols = columns(LAST - t)
                nc.gpsimd.tensor_scalar(clamped[:, :], rowsum[:, cols], 1.0, TINY, ALU.add, ALU.max).then_inc(pool_step, 1)
                nc.gpsimd.tensor_scalar(positive[:, :], rowsum[:, cols], 1.0, 0.0, ALU.add, ALU.is_gt).then_inc(pool_step, 1)
                pool.wait_ge(pool_step, 3 * t + 2)
                nc.gpsimd.tensor_tensor(power[:, :], clamped[:, :], neg_half[:, :], ALU.pow).then_inc(pool_step, 1)
                pool.wait_ge(pool_step, 3 * t + 3)
                nc.gpsimd.tensor_tensor(dinv[:, cols], power[:, :], positive[:, :], ALU.mult).then_inc(dinv_ready, 1)

            def inverse_deviation(e):
                pool.wait_ge(var_ready, e + 1)
                nc.gpsimd.tensor_tensor(vareps[:, :], meanvar[:, :, 1], eps[:, :], ALU.add).then_inc(pool_step, 1)
                pool.wait_ge(pool_step, 3 * NP + 1 + e)
                nc.gpsimd.tensor_tensor(rstd[:, :], vareps[:, :], neg_half[:, :], ALU.pow).then_inc(rstd_ready, 1)

            with pool.Fori(0, NP) as e:
                inverse_deviation(e)
            with pool.Fori(0, NP) as s:
                pool.wait_ge(x1_ready, NP)
                pool.wait_ge(proj_read, s + NP)
                nc.gpsimd.tensor_tensor(biased[:, :], feat[:, s, :], b1_sb[:, :], ALU.add).then_inc(biased_ready, 1)
                inverse_deviation(s + NP)

        @block.scalar
        def _(act):
            for dst, src in ((w0_sb, w0t), (w1_sb, w1), (b0_sb, b0), (b1_sb, b1), (beta_sb, beta)):
                act.dma_start(dst[:, :], src).then_inc(consts_in, 16)
            act.wait_ge(ident_done, 1)
            nc.scalar.activation(ident_r[:, :], ident[:, :], ACT.Copy).then_inc(ident_r_done, 1)

            def hi_half(q, h, slot, count):
                if h == 0:
                    act.wait_ge(block_in[slot], count)
                if not isinstance(q, int) or 2 * q + h >= NHI:
                    act.wait_ge(half_used, 2 * q + h - (NHI - 1))
                buf = (2 * hi_half.static + h) % NHI
                nc.scalar.activation(hi_a[:, buf, :], blocks[:, slot, h * HALF:(h + 1) * HALF], ACT.Copy).then_inc(hi_ready, 1)

            def hi_use(u, halves=(0, 1)):
                hi_half.static = u.index
                for h in halves:
                    hi_half(u.index, h, u.load.slot, u.load.arrived)

            def copy_out(e, bank_of, buf):
                if not isinstance(e, int) or e >= 2:
                    act.wait_ge(proj_ready, e - 1)
                else:
                    act.wait_ge(dinv_ready, NP)
                nc.scalar.activation(agg[:, buf, :], bank_of[:, :], ACT.Copy).then_inc(agg_ready, 1)

            for pre, post in use_stages:
                for u in pre + post:
                    if not u.native:
                        hi_use(u)
            for n, u in enumerate(final):
                act.wait_ge(native_used, u.index + 1)
                copy_out(n, bank[u.I], n % 2)

            def layer1_step(s, parity, first=False):
                for J in range(NP):
                    slot, count = arrival(s, J)
                    q = split_of(s, J)
                    hi_half.static = splits0 + J
                    hi_half(q, 0, slot, count)
                    if J == 1:
                        if first:
                            act.wait_ge(native_used, closing[-1].index + 1)
                        else:
                            act.wait_ge(half_used, 2 * split_of(s, 0))
                        copy_out(s + NP - 1, bank[LAST] if first else bank[1 - parity], 1 - parity)
                    hi_half(q, 1, slot, count)
                    if J == 3:
                        if first:
                            act.wait_ge(x1_ready, NP)
                        nc.scalar.activation(beta4[:, :], beta_sb[:, columns(s)], ACT.Copy).then_inc(act_step, 1)
                        act.wait_ge(act_step, s + 1)
                        for k in range(T):
                            last = nc.scalar.activation(self_f[:, k * F:(k + 1) * F], feat[:, s, k * F:(k + 1) * F],
                                                        ACT.Copy, scale=beta4[:, k:k + 1])
                        last.then_inc(self_ready, 1)
                    if J == 6 and not first and not (isinstance(s, int) and s == 0):
                        store(s - 1, 1 - parity)

            def store(s, buf):
                act.wait_ge(rows_ready, s + 1)
                act.dma_start(out_v[s, :, :], z[:, buf, :]).then_inc(stored[buf], 16)

            act.wait_ge(consts_in, 80)
            layer1_step(0, 0, first=True)
            layer1_step(1, 1)
            with act.Fori(0, NP // 2 - 1) as r:
                layer1_step(2 * r + 2, 0)
                layer1_step(2 * r + 3, 1)
            act.wait_ge(half_used, 2 * split_of(NP, 0))
            copy_out(2 * NP - 1, bank[1], 1)
            store(LAST, 1)
            act.wait_ge(stored[0], 16 * (NP // 2))
            act.wait_ge(stored[1], 16 * (NP // 2))

        @block.vector
        def _(vec):
            steps = [0, 0]

            def link(instruction):
                instruction.then_inc(vec_step, 1)
                steps[0] += 1
                vec.wait_ge(vec_step, steps[0] + steps[1])

            def degree(l):
                if l.degree_pos == 0:
                    return
                vec.wait_ge(block_in[l.slot], l.arrived)
                if l.degree_pos == 1:
                    other = load_stages[l.I][0]
                    vec.wait_ge(block_in[other.slot], other.arrived)
                    first = blocks[:, other.slot, :]
                else:
                    vec.wait_ge(degrees, degree_count(l.I, l.degree_pos) - 1)
                    first = part
                nc.vector.tensor_tensor(part, first, blocks[:, l.slot, :], ALU.add).then_inc(degrees, 1)

            def lo_half(q, h, slot, static):
                vec.wait_ge(hi_ready, 2 * q + h + 1)
                if not isinstance(q, int) or 2 * q + h >= NLO:
                    vec.wait_ge(half_used, 2 * q + h - (NLO - 1))
                hi = hi_a[:, (2 * static + h) % NHI, :].bitcast(f32)
                nc.vector.tensor_tensor(lo_a[:, (2 * static + h) % NLO, :], blocks[:, slot, h * HALF:(h + 1) * HALF],
                                        hi, ALU.subtract).then_inc(lo_ready, 1)

            def lo_use(u):
                for h in range(2):
                    lo_half(u.index, h, u.load.slot, u.index)

            def save_rowsum(t):
                vec.wait_ge(rowsum_ready, t + 1)
                nc.vector.tensor_copy(rowsum[:, columns(LAST - t)], bank[LAST][:, 0:T]).then_inc(rowsum_saved, 1)

            def scale_features(t):
                vec.wait_ge(x_in[t], 16)
                vec.wait_ge(dinv_ready, t + 1)
                y = scaled[:, NATIVE.index(t), :] if t in NATIVE else part[:, 0:T * F]
                for k in range(T):
                    last = nc.vector.tensor_scalar(y[:, k * F:(k + 1) * F], feat[:, LAST - t, k * F:(k + 1) * F],
                                                   dinv[:, columns(LAST - t)][:, k:k + 1], None, ALU.mult)
                if t in NATIVE:
                    last.then_inc(y_ready, 1)
                else:
                    link(last)
                    link(nc.vector.tensor_copy(hi_f[:, t, :], y))
                    nc.vector.tensor_tensor(lo_f[:, t, :], y, hi_f[:, t, :].bitcast(f32), ALU.subtract).then_inc(y_ready, 1)
                if t == 0:
                    vec.wait_ge(consts_in, 80)
                vec.wait_ge(y_ready, t + 1)
                link(nc.vector.tensor_tensor(feat[:, LAST - t, :], feat[:, LAST - t, :], b0_sb[:, :], ALU.add))

            def residual(e, proj_bank, features, factor, buf, next_scale=None):
                vec.wait_ge(proj_ready, e + 1)
                for k in range(T):
                    last = nc.vector.scalar_tensor_tensor(z[:, buf, k * F:(k + 1) * F], proj_bank[:, k * F:(k + 1) * F],
                                                          factor[:, k:k + 1], features[:, k * F:(k + 1) * F],
                                                          ALU.mult, ALU.add)
                last.then_inc(proj_read, 1)
                vec.wait_ge(proj_read, e + 1)
                for k in range(T):
                    last = nc.vector.bn_stats(stats[:, k, :], z[:, buf, k * F:(k + 1) * F])
                link(last)
                if next_scale is not None:
                    nc.vector.tensor_copy(scale4[:, :], scale[:, columns(next_scale)]).then_inc(scale_set, 1)
                for k in range(T):
                    last = nc.vector.bn_aggr(meanvar[:, k, :], stats[:, k, :])
                last.then_inc(var_ready, 1)

            def normalise(e, dst, buf):
                vec.wait_ge(var_ready, e + 1)
                vec.wait_ge(rstd_ready, e + 1)
                for k in range(T):
                    last = nc.vector.tensor_scalar(dst[:, k * F:(k + 1) * F], z[:, buf, k * F:(k + 1) * F],
                                                   meanvar[:, k, 0:1], rstd[:, k:k + 1], ALU.subtract, ALU.mult)
                return last

            def residual0(e):
                I = x1_order[e]
                residual(e, bank[I], feat[:, LAST - I, :], dinv[:, columns(LAST - I)], e % 2)

            def normalise0(e):
                I = x1_order[e]
                link(normalise(e, feat[:, LAST - I, :], e % 2))
                link(nc.vector.tensor_copy(hi_f[:, I, :], feat[:, LAST - I, :]))
                nc.vector.tensor_tensor(lo_f[:, I, :], feat[:, LAST - I, :], hi_f[:, I, :].bitcast(f32), ALU.subtract).then_inc(x1_ready, 1)

            vec.wait_ge(consts_set, 1)
            for t in range(NP):
                pre, post = use_stages[t]
                pending = [u for u in pre if not u.native]
                tail = [u for u in post if not u.native]
                for l in load_stages[t]:
                    while pending and pending[0].position < l.position:
                        lo_use(pending.pop(0))
                    if l.degree_pos is not None:
                        degree(l)
                        if pending and pending[0].load.number <= l.number:
                            lo_use(pending.pop(0))
                for u in pending + tail[:1]:
                    lo_use(u)
                save_rowsum(t)
                for u in tail[1:]:
                    lo_use(u)
                scale_features(t)
            link(nc.vector.tensor_tensor(scale[:, :], rowsum[:, :], beta_sb[:, :], ALU.add))
            link(nc.vector.reciprocal(scale[:, :], scale[:, :]))
            nc.vector.tensor_copy(scale4[:, :], scale[:, columns(0)]).then_inc(scale_set, 1)
            for n in range(NP - 1):
                residual0(n)
                normalise0(n)

            def layer1_step(s, parity, first=False):
                for J in range(NP):
                    slot = arrival(s, J)[0]
                    for h in range(2):
                        lo_half(split_of(s, J), h, slot, splits0 + J)
                    if J == 2:
                        residual0(LAST) if first else residual1(s - 1, 1 - parity)
                    if J == 3:
                        normalise0(LAST) if first else normalise1(s - 1, 1 - parity)

            def residual1(s, buf):
                vec.wait_ge(scale_set, s + 1)
                if not isinstance(s, int) or s >= STORES:
                    vec.wait_ge(stored[buf], store_count(s, buf))
                vec.wait_ge(biased_ready, s + 1)
                residual(s + NP, bank[2 + buf], biased[:, :], scale4, buf,
                         None if isinstance(s, int) and s == LAST else s + 1)

            def store_count(s, buf):
                return (s - buf) * 8

            def normalise1(s, buf):
                normalise(s + NP, z[:, buf, :], buf).then_inc(rows_ready, 1)

            layer1_step(0, 0, first=True)
            layer1_step(1, 1)
            before = steps[0]
            with vec.Fori(0, NP // 2 - 1) as r:
                steps[1] = r * 2
                layer1_step(2 * r + 2, 0)
                layer1_step(2 * r + 3, 1)
            assert steps[0] - before == 2
            steps[0], steps[1] = before + 2 * (NP // 2 - 1), 0
            residual1(LAST, 1)
            normalise1(LAST, 1)

        @block.tensor
        def _(pe):
            opened = set()

            def opens(b):
                if b in opened:
                    return False
                opened.add(b)
                return True

            def block_native(u, stop):
                pe.wait_ge(y_ready, u.J + 1)
                pe.wait_ge(block_in[u.load.slot], u.load.arrived)
                for k in range(T):
                    last = nc.tensor.matmul(bank[u.I][:, :], scaled[:, NATIVE.index(u.J), k * F:(k + 1) * F],
                                            blocks[:, u.load.slot, k * B:(k + 1) * B], start=opens(u.I),
                                            stop=stop and k == T - 1)
                last.then_inc(native_used, 1)

            def block_split(J, q, static, dst, start, stop):
                for h in range(2):
                    pe.wait_ge(lo_ready, 2 * q + h + 1)
                    for k in range(T // 2):
                        tile = (h * (T // 2) + k) * F
                        hf, lf = hi_f[:, J, tile:tile + F], lo_f[:, J, tile:tile + F]
                        ha = hi_a[:, (2 * static + h) % NHI, k * B:(k + 1) * B]
                        la = lo_a[:, (2 * static + h) % NLO, k * B:(k + 1) * B]
                        done = stop and h == 1 and k == T // 2 - 1
                        nc.tensor.matmul(dst[:, :], hf, ha, start=start and h == 0 and k == 0, stop=False)
                        nc.tensor.matmul(dst[:, :], hf, la, start=False, stop=False)
                        last = nc.tensor.matmul(dst[:, :], lf, ha, start=False, stop=done)
                    last.then_inc(half_used, 1)

            def add_self(t):
                pe.wait_ge(ident_r_done, 1)
                for k in range(T):
                    cols = bank[t][:, k * P:(k + 1) * P]
                    if t in NATIVE:
                        nc.tensor.matmul(cols, scaled[:, NATIVE.index(t), k * F:(k + 1) * F], ident[:, :], start=False, stop=False)
                    else:
                        for f in (hi_f, lo_f):
                            nc.tensor.matmul(cols, f[:, t, k * F:(k + 1) * F], ident_r[:, :], start=False, stop=False)

            def layer0_block(u, stop=False):
                pe.wait_ge(y_ready, u.J + 1)
                if u.native:
                    block_native(u, stop)
                else:
                    block_split(u.J, u.index, u.index, bank[u.I], opens(u.I), stop)
                if u.J == u.I and not stop:
                    add_self(u.I)

            def sum_degrees(t):
                pe.wait_ge(degrees, degree_count(t, NP - 1))
                if t >= 1:
                    pe.wait_ge(rowsum_saved, t)
                for g in range(T):
                    for k in range(T):
                        last = nc.tensor.matmul(bank[LAST][:, g:g + 1], part[:, k * B + g * P:k * B + (g + 1) * P],
                                                ones[:, :], start=k == 0, stop=k == T - 1)
                last.then_inc(rowsum_ready, 1)

            def project(e, dst, weights, buf):
                pe.wait_ge(agg_ready, e + 1)
                for k in range(T):
                    last = nc.tensor.matmul(dst[:, k * F:(k + 1) * F], agg[:, buf, k * P:(k + 1) * P],
                                            weights[:, :], start=True, stop=True)
                last.then_inc(proj_ready, 1)

            def project0(e):
                project(e, bank[x1_order[e]], w0_sb, e % 2)

            pe.wait_ge(consts_set, 1)
            pe.wait_ge(consts_in, 80)
            for t, (pre, post) in enumerate(use_stages):
                for u in pre:
                    layer0_block(u)
                sum_degrees(t)
                if t == LAST:
                    pe.wait_ge(rowsum_saved, NP)
                for u in post:
                    layer0_block(u)
            for n, u in enumerate(final):
                layer0_block(u, stop=True)
                if n >= 1:
                    project0(n - 1)
            for n, u in enumerate(closing):
                if u.J == LAST:
                    add_self(LAST)
                layer0_block(u, stop=u.J == LAST)
                if n == 0:
                    project0(NP - 2)

            def layer1_step(s, parity, first=False):
                acc = bank[parity]
                for J in range(NP):
                    if first:
                        pe.wait_ge(x1_ready, x1_order.index(J) + 1)
                    if J == LAST:
                        pe.wait_ge(self_ready, s + 1)
                        for k in range(T):
                            nc.tensor.matmul(acc[:, k * P:(k + 1) * P], self_f[:, k * F:(k + 1) * F], ident[:, :],
                                             start=False, stop=False)
                    block_split(J, split_of(s, J), splits0 + J, acc, J == 0, J == LAST)
                    if J == 1:
                        if first:
                            project0(LAST)
                        else:
                            if not isinstance(s, int) or s >= 3:
                                pe.wait_ge(proj_read, s + NP - 2)
                            project(s + NP - 1, bank[3 - parity], w1_sb, 1 - parity)

            pe.wait_ge(proj_read, NP - 1)
            layer1_step(0, 0, first=True)
            layer1_step(1, 1)
            with pe.Fori(0, NP // 2 - 1) as r:
                layer1_step(2 * r + 2, 0)
                layer1_step(2 * r + 3, 1)
            project(2 * NP - 1, bank[3], w1_sb, 1)


def kernel(x, adj, L0_gnn_W, L0_gnn_b, L1_gnn_kernel, L1_gnn_bias, L1_gnn_beta):
    import numpy as np
    import concourse.bacc as bacc
    from concourse.bass_utils import run_bass_kernel_spmd

    a = np.asarray(adj).reshape(NP, P, T, NP, P, T)
    arrays = {
        "x_in": np.ascontiguousarray(x),
        "adj_in": np.ascontiguousarray(a.transpose(0, 3, 4, 5, 2, 1)).reshape(NP, NP, P, T * B),
        "w0t_in": np.ascontiguousarray(np.asarray(L0_gnn_W).T),
        "b0_in": np.ascontiguousarray(np.tile(np.asarray(L0_gnn_b), (P, T))),
        "w1_in": np.ascontiguousarray(L1_gnn_kernel),
        "b1_in": np.ascontiguousarray(np.tile(np.asarray(L1_gnn_bias), (P, T))),
        "beta_in": np.ascontiguousarray(np.asarray(L1_gnn_beta).reshape(NP, P, T).transpose(1, 0, 2)).reshape(P, NP * T),
    }
    nc = bacc.Bacc("TRN2", target_bir_lowering=False, num_devices=1)
    f32 = mybir.dt.float32
    aps = [nc.dram_tensor(k, v.shape, f32, kind="ExternalInput").ap() for k, v in arrays.items()]
    out = nc.dram_tensor("out", (N, F), f32, kind="ExternalOutput").ap()
    two_gnn_layers(nc, *aps, out)
    r = run_bass_kernel_spmd(nc, [arrays], core_ids=[0])
    return r.results[0]["out"]
```

```python
from contextlib import ExitStack

import concourse.bass as bass
from concourse import mybir

N = 4096
F = 128
P = 128
NP = 8
B = N // NP
T = B // P
HALF = T // 2 * B
SLOTS = 11
STAGING_SLOTS = 4
RESULT_SLOTS = 4
KEEP = 4
SAVE_AT, SCALE_AT = 2, 3
AHEAD = 3
NATIVE = list(range(8))
NHI, NLO = 4, 4
EPS = 1e-5
TINY = 1.2e-38
LAST = NP - 1
FINAL = [I for I in range(LAST) if LAST - I <= KEEP] + [I for I in range(LAST) if LAST - I > KEEP]
STORES = 2


class Use:

    def __init__(self, J, I):
        self.J, self.I, self.native = J, I, J in NATIVE


class Load:

    def __init__(self, J, I, degree_pos):
        self.J, self.I, self.degree_pos = J, I, degree_pos
        self.waits = {}


def layer0_uses():
    stages = []
    for t in range(LAST):
        first = list(range(min(2, t - 1))) if t > 1 else []
        late = [t - 2, t - 1] if t == LAST - 1 else []
        rest = [J for J in range(t) if J not in first + late]
        stages.append([Use(J, t) for J in first] + [Use(t - 1, I) for I in range(t - 1, -1, -1)] + [Use(J, t) for J in rest])
    t = LAST
    stages.append([Use(J, t - 1) for J in late] + [Use(t - 1, I) for I in range(t - 1, -1, -1)])
    behind = [Use(J, t) for J in (5, 6, 0, 1)]
    final = [Use(t, I) for I in FINAL]
    closing = [Use(J, t) for J in (2, 3, 4, 7)]
    return stages, behind, final, closing


def layer0_loads():
    stages = []
    for t in range(NP):
        loads = [Load(J, t, J) for J in range(t)]
        again = [Load(t - 1, I, None) for I in range(t - 1, -1, -1) if t - 1 - I > KEEP]
        loads = loads[:2] + again + loads[2:]
        loads += [Load(J, t, J) for J in range(t, NP)]
        stages.append(loads)
    again = [Load(LAST, I, None) for I in FINAL if LAST - I > KEEP]
    return stages, again


def degree_count(t, pos):
    return (NP - 1) * t + max(pos, 1)


def place_blocks():
    stages, behind, final, closing = layer0_uses()
    load_stages, again = layer0_loads()
    uses = [u for stage in stages for u in stage] + behind + final + closing
    loads = [l for st in load_stages for l in st] + again
    native = split = 0
    for n, u in enumerate(uses):
        u.position = n
        if u.native:
            u.index, native = native, native + 1
        else:
            u.index, split = split, split + 1
    reuse = [Use(J, LAST) for J in range(NP)]
    for J, u in enumerate(reuse):
        u.native, u.index, u.position = False, split + J, len(uses) + J
    next_panel = [Load(J, LAST - 1, None) for J in range(NP)]
    position_of = {(u.J, u.I): u.position for u in uses + reuse}
    staging_from = next(u.position for u in uses + reuse if not u.native) - AHEAD
    results_from = final[0].position
    until = {}
    for n in range(SLOTS + STAGING_SLOTS + RESULT_SLOTS):
        until[n] = len(uses) + NP + 1 if n < SLOTS else staging_from if n < SLOTS + STAGING_SLOTS else results_from
    free = [(s, {}) for s in sorted(until, reverse=True)]
    held, dropped, queue = {}, [], uses + reuse
    taken = {n: 0 for n in until}
    position = 0
    staging_waits = {"native": 0, "degrees": 0}
    for n, l in enumerate(loads + next_panel):
        drops = l.degree_pos is not None and l.J - l.I > KEEP
        last_use = next((u.position for u in stages[l.I + 1]), 0) if drops else position_of[(l.J, l.I)]
        if n >= len(loads):
            last_use = len(uses) + NP
        while True:
            fits = [f for f in free if last_use < until[f[0]]]
            if fits:
                break
            if dropped and dropped[0].degree_pos >= 1:
                d = dropped.pop(0)
                free.append((d.slot, {"degrees": degree_count(d.I, d.degree_pos)}))
                continue
            u = queue[position]
            b = held[(u.J, u.I)]
            u.load = b
            position += 1
            if u.I == LAST and u in uses:
                continue
            waits = {"native": u.index + 1} if u.native else {"split": 2 * u.index + 2}
            if b.degree_pos is not None:
                waits["degrees"] = degree_count(b.I, b.degree_pos)
            free.append((b.slot, waits))
            del held[(u.J, u.I)]
        free.remove(fits[0])
        l.slot, l.waits = fits[0]
        l.number, l.position = n, position
        taken[l.slot] += 1
        l.arrived = 16 * taken[l.slot]
        if SLOTS <= l.slot < SLOTS + STAGING_SLOTS and l.degree_pos is not None:
            staging_waits["degrees"] = max(staging_waits["degrees"], degree_count(l.I, l.degree_pos))
        if drops:
            dropped.append(l)
        else:
            held[(l.J, l.I)] = l
    for u in queue[position:]:
        u.load = held[(u.J, u.I)]
    staging_waits["native"] = sum(u.native for u in uses[:staging_from])
    return stages, behind, final, closing, load_stages, again, reuse, next_panel, split, staging_waits


def two_gnn_layers(nc, x, adj, w0t, b0, w1, b1, beta, out):
    f32, f32r = mybir.dt.float32, mybir.dt.float32r
    ALU, ACT = mybir.AluOpType, mybir.ActivationFunctionType
    stages, behind, final, closing, load_stages, again, reuse, next_panel, splits0, staging_waits = place_blocks()
    ring = [l.slot for l in next_panel]
    arrived1 = [l.arrived for l in next_panel]

    ctx = ExitStack()
    with ctx:
        def sb(name, shape, dt=f32):
            return ctx.enter_context(nc.sbuf_tensor(name, shape, dt))

        def sem(name):
            return ctx.enter_context(nc.semaphore(name))

        blocks = sb("blocks", [P, SLOTS, T * B])
        feat = sb("feat", [P, NP, T * F])
        split_y = [J for J in range(NP) if J not in NATIVE]
        with nc.sbuf_tensor("result_slots", [P, RESULT_SLOTS, T * B], f32) as result_slots:
            pass
        hi_x, lo_x = (sb(n, [P, len(NATIVE), T * F], f32r) for n in ("hi_x", "lo_x"))
        scaled = sb("scaled", [P, len(NATIVE), T * F])
        with nc.sbuf_tensor("staging_slots", [P, STAGING_SLOTS, T * B], f32) as staging_slots:
            pass
        hi_a = sb("hi_a", [P, NHI, HALF], f32r)
        lo_a = sb("lo_a", [P, NLO, HALF], f32r)
        work = sb("work", [P, T * B])
        fold_f = sb("fold_f", [P, B])
        part = work[:, :]
        z = work[:, 0:2 * B].rearrange("p (s c) -> p s c", s=2)
        agg = work[:, 2 * B:4 * B].rearrange("p (s c) -> p s c", s=2)
        w0_sb, w1_sb = sb("w0_sb", [F, F]), sb("w1_sb", [F, F])
        b0_sb, b1_sb = sb("b0_sb", [P, T * F]), sb("b1_sb", [P, T * F])
        ident, ident_r = sb("ident", [P, P]), sb("ident_r", [P, P], f32r)
        self_f = sb("self_f", [P, T * F])
        biased = sb("biased", [P, T * F])
        ones = sb("ones", [P, 1])
        neg_half = sb("neg_half", [P, T])
        beta_sb, rowsum = sb("beta_sb", [P, NP * T]), sb("rowsum", [P, NP * T])
        dinv = sb("dinv", [P, NP * T])
        scale = sb("scale", [P, NP * T])
        positive, clamped, power = sb("positive", [P, T]), sb("clamped", [P, T]), sb("power", [P, T])
        scale4, beta4 = sb("scale4", [P, T]), sb("beta4", [P, T])
        stats, meanvar = sb("stats", [P, T, 6]), sb("meanvar", [P, T, 2])
        eps, zeros = sb("eps", [P, T]), sb("zeros", [P, T])
        vareps, rstd = sb("vareps", [P, T]), sb("rstd", [P, T])
        negmean, shift = sb("negmean", [P, T]), sb("shift", [P, T])

        bank = [ctx.enter_context(nc.psum_tensor(f"bank{i}", [P, B], f32)) for i in range(NP)]

        block_in = [sem(f"block_in{s}") for s in range(SLOTS + STAGING_SLOTS + RESULT_SLOTS)]
        x_in = [sem(f"x_in{t}") for t in range(NP)]
        consts_in = sem("consts_in")
        ident_zero, consts_set, ident_done, ident_r_done = (sem(n) for n in ("ident_zero", "consts_set", "ident_done", "ident_r_done"))
        degrees = sem("degrees")
        folded = sem("folded")
        rowsum_ready = sem("rowsum_ready")
        rowsum_saved = sem("rowsum_saved")
        pool_step, vec_step, act_step = sem("pool_step"), sem("vec_step"), sem("act_step")
        dinv_ready = sem("dinv_ready")
        y_ready = sem("y_ready")
        hi_ready, lo_ready = sem("hi_ready"), sem("lo_ready")
        half_used = sem("half_used")
        native_used = sem("native_used")
        agg_ready = sem("agg_ready")
        proj_ready, proj_read = sem("proj_ready"), sem("proj_read")
        var_ready, rstd_ready = sem("var_ready"), sem("rstd_ready")
        normed = sem("normed")
        hi_x_ready = sem("hi_x_ready")
        x1_ready = sem("x1_ready")
        self_ready = sem("self_ready")
        biased_ready = sem("biased_ready")
        scale_set = sem("scale_set")
        stored = [sem(f"stored{i}") for i in range(STORES)]

        x_v = x.rearrange("(b p k) f -> b p (k f)", b=NP, p=P)
        out_v = out.rearrange("(b p k) f -> b p (k f)", b=NP, p=P)
        adj_flat = adj.rearrange("i j p c -> (i j p c)")
        x1_order = FINAL + [LAST]

        def slot_of(n):
            if n < SLOTS:
                return blocks[:, n, :]
            n -= SLOTS
            return staging_slots[:, n, :] if n < STAGING_SLOTS else result_slots[:, n - STAGING_SLOTS, :]

        def hi(J):
            return hi_x[:, NATIVE.index(J), :] if J in NATIVE else hi_y[:, split_y.index(J), :]

        def lo(J):
            return lo_x[:, NATIVE.index(J), :] if J in NATIVE else lo_y[:, split_y.index(J), :]

        def split_of(s, J):
            return splits0 + NP * s + J

        def columns(s):
            if isinstance(s, int):
                return slice(s * T, (s + 1) * T)
            return bass.ds(s * T, T)

        def arrival(s, J):
            if isinstance(s, int) and s == 0:
                return reuse[J].load.slot, reuse[J].load.arrived
            return ring[J], arrived1[J] + (s - 1) * 16

        block = ctx.enter_context(nc.Block())

        @block.sync
        def _(sync):
            def load(l):
                if "degrees" in l.waits:
                    sync.wait_ge(degrees, l.waits["degrees"])
                if "native" in l.waits:
                    sync.wait_ge(native_used, l.waits["native"])
                if "split" in l.waits:
                    sync.wait_ge(lo_ready, l.waits["split"])
                sync.dma_start(slot_of(l.slot), adj[LAST - l.I, LAST - l.J, :, :]).then_inc(block_in[l.slot], 16)

            for t in range(NP):
                for n, l in enumerate(load_stages[t]):
                    load(l)
                    if n == NP - 3:
                        sync.dma_start(feat[:, LAST - t, :], x_v[LAST - t, :, :]).then_inc(x_in[t], 16)
            for l in again + next_panel:
                load(l)
            with sync.Fori(0, NP // 2 - 1) as r:
                for u in range(2):
                    s = 2 * r + (2 + u)
                    for J in range(NP):
                        start = sync.snap((s * NP + (LAST - J)) * (P * T * B))
                        source = adj_flat[bass.ds(start, P * T * B)].rearrange("(p c) -> p c", p=P)
                        sync.wait_ge(lo_ready, 2 * split_of(s - 1, J) + 2)
                        sync.dma_start(blocks[:, ring[J], :], source).then_inc(block_in[ring[J]], 16)

        @block.gpsimd
        def _(pool):
            nc.gpsimd.memset(ident[:, :], 0.0).then_inc(ident_zero, 1)
            nc.gpsimd.memset(ones[:, :], 1.0).then_inc(consts_set, 1)
            nc.gpsimd.memset(neg_half[:, :], -0.5).then_inc(consts_set, 1)
            nc.gpsimd.memset(eps[:, :], EPS).then_inc(consts_set, 1)
            nc.gpsimd.memset(zeros[:, :], 0.0).then_inc(consts_set, 1)
            pool.wait_ge(ident_zero, 1)
            nc.gpsimd.affine_select(out=ident[:, :], in_=ident[:, :], compare_op=ALU.not_equal, fill=1.0,
                                    base=0, pattern=[[-1, P]], channel_multiplier=1).then_inc(ident_done, 1)
            pool.wait_ge(consts_set, 4)
            for t in range(NP):
                pool.wait_ge(rowsum_saved, t + 1)
                cols = columns(LAST - t)
                nc.gpsimd.tensor_scalar(clamped[:, :], rowsum[:, cols], 1.0, TINY, ALU.add, ALU.max).then_inc(pool_step, 1)
                nc.gpsimd.tensor_scalar(positive[:, :], rowsum[:, cols], 1.0, 0.0, ALU.add, ALU.is_gt).then_inc(pool_step, 1)
                pool.wait_ge(pool_step, 3 * t + 2)
                nc.gpsimd.tensor_tensor(power[:, :], clamped[:, :], neg_half[:, :], ALU.pow).then_inc(pool_step, 1)
                pool.wait_ge(pool_step, 3 * t + 3)
                nc.gpsimd.tensor_tensor(dinv[:, cols], power[:, :], positive[:, :], ALU.mult).then_inc(dinv_ready, 1)

            def deviation(e):
                steps = 3 * NP + 3 * e
                pool.wait_ge(var_ready, e + 1)
                nc.gpsimd.tensor_tensor(vareps[:, :], meanvar[:, :, 1], eps[:, :], ALU.add).then_inc(pool_step, 1)
                nc.gpsimd.tensor_tensor(negmean[:, :], zeros[:, :], meanvar[:, :, 0], ALU.subtract).then_inc(pool_step, 1)
                if not isinstance(e, int) or e >= 1:
                    pool.wait_ge(normed, e)
                pool.wait_ge(pool_step, steps + 2)
                nc.gpsimd.tensor_tensor(rstd[:, :], vareps[:, :], neg_half[:, :], ALU.pow).then_inc(pool_step, 1)
                pool.wait_ge(pool_step, steps + 3)
                nc.gpsimd.tensor_tensor(shift[:, :], negmean[:, :], rstd[:, :], ALU.mult).then_inc(rstd_ready, 1)

            deviation(0)
            with pool.Fori(1, NP) as e:
                deviation(e)
            with pool.Fori(0, NP) as s:
                pool.wait_ge(x1_ready, NP)
                pool.wait_ge(proj_read, s + NP)
                nc.gpsimd.tensor_tensor(biased[:, :], feat[:, s, :], b1_sb[:, :], ALU.add).then_inc(biased_ready, 1)
                deviation(s + NP)

        @block.scalar
        def _(act):
            for dst, src in ((w0_sb, w0t), (w1_sb, w1), (b0_sb, b0), (b1_sb, b1), (beta_sb, beta)):
                act.dma_start(dst[:, :], src).then_inc(consts_in, 16)
            act.wait_ge(ident_done, 1)
            nc.scalar.activation(ident_r[:, :], ident[:, :], ACT.Copy).then_inc(ident_r_done, 1)

            def hi_half(q, h, slot, count):
                if h == 0:
                    act.wait_ge(block_in[slot], count)
                if not isinstance(q, int) or 2 * q + h >= NHI:
                    act.wait_ge(half_used, 2 * q + h - (NHI - 1))
                buf = (2 * hi_half.static + h) % NHI
                nc.scalar.activation(hi_a[:, buf, :], slot_of(slot)[:, h * HALF:(h + 1) * HALF], ACT.Copy).then_inc(hi_ready, 1)

            def hi_use(u, halves=(0, 1)):
                hi_half.static = u.index
                for h in halves:
                    hi_half(u.index, h, u.load.slot, u.load.arrived)

            def copy_out(e, bank_of, buf):
                if not isinstance(e, int) or e >= 2:
                    act.wait_ge(proj_ready, e - 1)
                else:
                    act.wait_ge(dinv_ready, NP)
                nc.scalar.activation(agg[:, buf, :], bank_of[:, :], ACT.Copy).then_inc(agg_ready, 1)

            def normalise(e, dst, buf):
                act.wait_ge(rstd_ready, e + 1)
                for k in range(T):
                    last = nc.scalar.activation(dst[:, k * F:(k + 1) * F], z[:, buf, k * F:(k + 1) * F], ACT.Identity,
                                                bias=shift[:, k:k + 1], scale=rstd[:, k:k + 1])
                last.then_inc(normed, 1)

            def normalise0(e):
                I = x1_order[e]
                normalise(e, feat[:, LAST - I, :], e % 2)
                act.wait_ge(normed, e + 1)
                nc.scalar.activation(hi(I), feat[:, LAST - I, :], ACT.Copy).then_inc(hi_x_ready, 1)

            for n, u in enumerate(final):
                act.wait_ge(native_used, u.index + 1)
                copy_out(n, bank[u.I], n % 2)
                if n >= 1:
                    normalise0(n - 1)
            normalise0(NP - 2)

            def layer1_step(s, parity, first=False):
                for J in range(NP):
                    slot, count = arrival(s, J)
                    q = split_of(s, J)
                    hi_half.static = splits0 + J
                    hi_half(q, 0, slot, count)
                    if J == 1:
                        if first:
                            act.wait_ge(native_used, closing[-1].index + 1)
                        else:
                            act.wait_ge(half_used, 2 * split_of(s, 0))
                        copy_out(s + NP - 1, bank[LAST] if first else bank[1 - parity], 1 - parity)
                    hi_half(q, 1, slot, count)
                    if J == 4:
                        normalise0(LAST) if first else normalise(s - 1 + NP, z[:, 1 - parity, :], 1 - parity)
                    if J == 5:
                        nc.scalar.activation(beta4[:, :], beta_sb[:, columns(s)], ACT.Copy).then_inc(act_step, 1)
                        act.wait_ge(act_step, s + 1)
                        for k in range(T):
                            last = nc.scalar.activation(self_f[:, k * F:(k + 1) * F], feat[:, s, k * F:(k + 1) * F],
                                                        ACT.Copy, scale=beta4[:, k:k + 1])
                        last.then_inc(self_ready, 1)
                    if J == 6 and not first and not (isinstance(s, int) and s == 0):
                        store(s - 1, 1 - parity)

            def store(s, buf):
                act.wait_ge(normed, s + NP + 1)
                act.dma_start(out_v[s, :, :], z[:, buf, :]).then_inc(stored[buf], 16)

            act.wait_ge(consts_in, 80)
            act.wait_ge(native_used, staging_waits["native"])
            act.wait_ge(degrees, staging_waits["degrees"])
            layer1_step(0, 0, first=True)
            layer1_step(1, 1)
            with act.Fori(0, NP // 2 - 1) as r:
                layer1_step(2 * r + 2, 0)
                layer1_step(2 * r + 3, 1)
            act.wait_ge(half_used, 2 * split_of(NP, 0))
            copy_out(2 * NP - 1, bank[1], 1)
            normalise(2 * NP - 1, z[:, 1, :], 1)
            store(LAST, 1)
            act.wait_ge(stored[0], 16 * (NP // 2))
            act.wait_ge(stored[1], 16 * (NP // 2))

        @block.vector
        def _(vec):
            steps = [0, 0]

            def link(instruction):
                instruction.then_inc(vec_step, 1)
                steps[0] += 1
                vec.wait_ge(vec_step, steps[0] + steps[1])

            def degree(l):
                if l.degree_pos == 0:
                    return
                vec.wait_ge(block_in[l.slot], l.arrived)
                if l.degree_pos == 1:
                    if l.I >= 1:
                        vec.wait_ge(folded, l.I)
                    other = load_stages[l.I][0]
                    vec.wait_ge(block_in[other.slot], other.arrived)
                    first = slot_of(other.slot)
                else:
                    vec.wait_ge(degrees, degree_count(l.I, l.degree_pos) - 1)
                    first = part
                nc.vector.tensor_tensor(part, first, slot_of(l.slot), ALU.add).then_inc(degrees, 1)

            def lo_half(q, h, slot, static):
                vec.wait_ge(hi_ready, 2 * q + h + 1)
                if not isinstance(q, int) or 2 * q + h >= NLO:
                    vec.wait_ge(half_used, 2 * q + h - (NLO - 1))
                hi_part = hi_a[:, (2 * static + h) % NHI, :].bitcast(f32)
                nc.vector.tensor_tensor(lo_a[:, (2 * static + h) % NLO, :], slot_of(slot)[:, h * HALF:(h + 1) * HALF],
                                        hi_part, ALU.subtract).then_inc(lo_ready, 1)

            def lo_use(u):
                for h in range(2):
                    lo_half(u.index, h, u.load.slot, u.index)

            def fold(t):
                vec.wait_ge(degrees, degree_count(t, NP - 1))
                link(nc.vector.tensor_tensor(part[:, 0:2 * B], part[:, 0:2 * B], part[:, 2 * B:4 * B], ALU.add))
                nc.vector.tensor_tensor(fold_f[:, :], part[:, 0:B], part[:, B:2 * B], ALU.add).then_inc(folded, 1)

            def save_rowsum(t):
                vec.wait_ge(rowsum_ready, t + 1)
                nc.vector.tensor_copy(rowsum[:, columns(LAST - t)], bank[LAST][:, 0:T]).then_inc(rowsum_saved, 1)

            def scale_features(t):
                vec.wait_ge(x_in[t], 16)
                vec.wait_ge(dinv_ready, t + 1)
                y = scaled[:, NATIVE.index(t), :] if t in NATIVE else fold_f[:, :]
                for k in range(T):
                    last = nc.vector.tensor_scalar(y[:, k * F:(k + 1) * F], feat[:, LAST - t, k * F:(k + 1) * F],
                                                   dinv[:, columns(LAST - t)][:, k:k + 1], None, ALU.mult)
                if t in NATIVE:
                    last.then_inc(y_ready, 1)
                else:
                    link(last)
                    link(nc.vector.tensor_copy(hi(t), y))
                    nc.vector.tensor_tensor(lo(t), y, hi(t).bitcast(f32), ALU.subtract).then_inc(y_ready, 1)
                if t == 0:
                    vec.wait_ge(consts_in, 80)
                vec.wait_ge(y_ready, t + 1)
                link(nc.vector.tensor_tensor(feat[:, LAST - t, :], feat[:, LAST - t, :], b0_sb[:, :], ALU.add))

            def residual(e, proj_bank, features, factor, buf, next_scale=None):
                if not isinstance(e, int) or e >= 1:
                    vec.wait_ge(rstd_ready, e)
                if not isinstance(e, int) or e >= 2:
                    vec.wait_ge(normed, e - 1)
                vec.wait_ge(proj_ready, e + 1)
                for k in range(T):
                    last = nc.vector.scalar_tensor_tensor(z[:, buf, k * F:(k + 1) * F], proj_bank[:, k * F:(k + 1) * F],
                                                          factor[:, k:k + 1], features[:, k * F:(k + 1) * F],
                                                          ALU.mult, ALU.add)
                last.then_inc(proj_read, 1)
                vec.wait_ge(proj_read, e + 1)
                for k in range(T):
                    last = nc.vector.bn_stats(stats[:, k, :], z[:, buf, k * F:(k + 1) * F])
                link(last)
                if next_scale is not None:
                    nc.vector.tensor_copy(scale4[:, :], scale[:, columns(next_scale)]).then_inc(scale_set, 1)
                for k in range(T):
                    last = nc.vector.bn_aggr(meanvar[:, k, :], stats[:, k, :])
                last.then_inc(var_ready, 1)

            def residual0(e):
                I = x1_order[e]
                residual(e, bank[I], feat[:, LAST - I, :], dinv[:, columns(LAST - I)], e % 2)

            def split0(e):
                I = x1_order[e]
                vec.wait_ge(hi_x_ready, e + 1)
                nc.vector.tensor_tensor(lo(I), feat[:, LAST - I, :], hi(I).bitcast(f32), ALU.subtract).then_inc(x1_ready, 1)

            vec.wait_ge(consts_set, 1)
            early = []
            for t in range(NP):
                pending = [u for u in stages[t] if not u.native and u not in early]
                chain = [(SAVE_AT, save_rowsum), (SCALE_AT, scale_features)] if t >= 1 else []
                needs_y = [u.position for u in stages[t] if u.J == t - 1][:1]
                for n, l in enumerate(load_stages[t]):
                    while chain and (n >= chain[0][0] or l.position > needs_y[0]):
                        chain.pop(0)[1](t - 1)
                    while pending and pending[0].position < l.position:
                        lo_use(pending.pop(0))
                    if l.degree_pos is not None:
                        degree(l)
                        if pending and not chain and pending[0].load.number <= l.number:
                            lo_use(pending.pop(0))
                fold(t)
                for u in pending:
                    lo_use(u)
            save_rowsum(LAST)
            scale_features(LAST)
            link(nc.vector.tensor_tensor(scale[:, :], rowsum[:, :], beta_sb[:, :], ALU.add))
            link(nc.vector.reciprocal(scale[:, :], scale[:, :]))
            nc.vector.tensor_copy(scale4[:, :], scale[:, columns(0)]).then_inc(scale_set, 1)
            for n in range(NP - 1):
                residual0(n)
                if n >= 1:
                    split0(n - 1)
            split0(NP - 2)

            def layer1_step(s, parity, first=False):
                for J in range(NP):
                    slot = arrival(s, J)[0]
                    for h in range(2):
                        lo_half(split_of(s, J), h, slot, splits0 + J)
                    if J == 2:
                        residual0(LAST) if first else residual1(s - 1, 1 - parity)
                    if J == 5 and first:
                        split0(LAST)

            def residual1(s, buf):
                vec.wait_ge(scale_set, s + 1)
                if not isinstance(s, int) or s >= STORES:
                    vec.wait_ge(stored[buf], store_count(s, buf))
                vec.wait_ge(biased_ready, s + 1)
                residual(s + NP, bank[2 + buf], biased[:, :], scale4, buf,
                         None if isinstance(s, int) and s == LAST else s + 1)

            def store_count(s, buf):
                return (s - buf) * 8

            layer1_step(0, 0, first=True)
            layer1_step(1, 1)
            before = steps[0]
            with vec.Fori(0, NP // 2 - 1) as r:
                steps[1] = r * 2
                layer1_step(2 * r + 2, 0)
                layer1_step(2 * r + 3, 1)
            assert steps[0] - before == 2
            steps[0], steps[1] = before + 2 * (NP // 2 - 1), 0
            residual1(LAST, 1)

        @block.tensor
        def _(pe):
            opened = set()

            def opens(b):
                if b in opened:
                    return False
                opened.add(b)
                return True

            def block_native(u, stop):
                pe.wait_ge(y_ready, u.J + 1)
                pe.wait_ge(block_in[u.load.slot], u.load.arrived)
                for k in range(T):
                    last = nc.tensor.matmul(bank[u.I][:, :], scaled[:, NATIVE.index(u.J), k * F:(k + 1) * F],
                                            slot_of(u.load.slot)[:, k * B:(k + 1) * B], start=opens(u.I),
                                            stop=stop and k == T - 1)
                last.then_inc(native_used, 1)

            def block_split(J, q, static, dst, start, stop):
                for h in range(2):
                    pe.wait_ge(lo_ready, 2 * q + h + 1)
                    for k in range(T // 2):
                        tile = (h * (T // 2) + k) * F
                        hf, lf = hi(J)[:, tile:tile + F], lo(J)[:, tile:tile + F]
                        ha = hi_a[:, (2 * static + h) % NHI, k * B:(k + 1) * B]
                        la = lo_a[:, (2 * static + h) % NLO, k * B:(k + 1) * B]
                        done = stop and h == 1 and k == T // 2 - 1
                        nc.tensor.matmul(dst[:, :], hf, ha, start=start and h == 0 and k == 0, stop=False)
                        nc.tensor.matmul(dst[:, :], hf, la, start=False, stop=False)
                        last = nc.tensor.matmul(dst[:, :], lf, ha, start=False, stop=done)
                    last.then_inc(half_used, 1)

            def add_self(t):
                pe.wait_ge(ident_r_done, 1)
                for k in range(T):
                    cols = bank[t][:, k * P:(k + 1) * P]
                    if t in NATIVE:
                        nc.tensor.matmul(cols, scaled[:, NATIVE.index(t), k * F:(k + 1) * F], ident[:, :], start=False, stop=False)
                    else:
                        for f in (hi(t), lo(t)):
                            nc.tensor.matmul(cols, f[:, k * F:(k + 1) * F], ident_r[:, :], start=False, stop=False)

            def layer0_block(u, stop=False):
                pe.wait_ge(y_ready, u.J + 1)
                if u.native:
                    block_native(u, stop)
                else:
                    block_split(u.J, u.index, u.index, bank[u.I], opens(u.I), stop)
                if u.J == u.I and not stop:
                    add_self(u.I)

            def sum_degrees(t):
                pe.wait_ge(folded, t + 1)
                if t >= 1:
                    pe.wait_ge(rowsum_saved, t)
                for g in range(T):
                    last = nc.tensor.matmul(bank[LAST][:, g:g + 1], fold_f[:, g * P:(g + 1) * P], ones[:, :],
                                            start=True, stop=True)
                last.then_inc(rowsum_ready, 1)

            def project(e, dst, weights, buf):
                pe.wait_ge(agg_ready, e + 1)
                for k in range(T):
                    last = nc.tensor.matmul(dst[:, k * F:(k + 1) * F], agg[:, buf, k * P:(k + 1) * P],
                                            weights[:, :], start=True, stop=True)
                last.then_inc(proj_ready, 1)

            def project0(e):
                project(e, bank[x1_order[e]], w0_sb, e % 2)

            pe.wait_ge(consts_set, 1)
            pe.wait_ge(consts_in, 80)
            for t, stage in enumerate(stages):
                for u in stage:
                    layer0_block(u)
                sum_degrees(t)
            pe.wait_ge(rowsum_saved, NP)
            for u in behind:
                layer0_block(u)
            for n, u in enumerate(final):
                layer0_block(u, stop=True)
                if n >= 1:
                    project0(n - 1)
            for n, u in enumerate(closing):
                if u.J == LAST:
                    add_self(LAST)
                layer0_block(u, stop=u.J == LAST)
                if n == 0:
                    project0(NP - 2)

            def layer1_step(s, parity, first=False):
                acc = bank[parity]
                for J in range(NP):
                    if first:
                        pe.wait_ge(x1_ready, x1_order.index(J) + 1)
                    if J == LAST:
                        pe.wait_ge(self_ready, s + 1)
                        for k in range(T):
                            nc.tensor.matmul(acc[:, k * P:(k + 1) * P], self_f[:, k * F:(k + 1) * F], ident[:, :],
                                             start=False, stop=False)
                    block_split(J, split_of(s, J), splits0 + J, acc, J == 0, J == LAST)
                    if J == 1:
                        if first:
                            project0(LAST)
                        else:
                            if not isinstance(s, int) or s >= 3:
                                pe.wait_ge(proj_read, s + NP - 2)
                            project(s + NP - 1, bank[3 - parity], w1_sb, 1 - parity)

            pe.wait_ge(proj_read, NP - 1)
            layer1_step(0, 0, first=True)
            layer1_step(1, 1)
            with pe.Fori(0, NP // 2 - 1) as r:
                layer1_step(2 * r + 2, 0)
                layer1_step(2 * r + 3, 1)
            project(2 * NP - 1, bank[3], w1_sb, 1)


def kernel(x, adj, L0_gnn_W, L0_gnn_b, L1_gnn_kernel, L1_gnn_bias, L1_gnn_beta):
    import numpy as np
    import concourse.bacc as bacc
    from concourse.bass_utils import run_bass_kernel_spmd

    a = np.asarray(adj).reshape(NP, P, T, NP, P, T)
    arrays = {
        "x_in": np.ascontiguousarray(x),
        "adj_in": np.ascontiguousarray(a.transpose(0, 3, 4, 5, 2, 1)).reshape(NP, NP, P, T * B),
        "w0t_in": np.ascontiguousarray(np.asarray(L0_gnn_W).T),
        "b0_in": np.ascontiguousarray(np.tile(np.asarray(L0_gnn_b), (P, T))),
        "w1_in": np.ascontiguousarray(L1_gnn_kernel),
        "b1_in": np.ascontiguousarray(np.tile(np.asarray(L1_gnn_bias), (P, T))),
        "beta_in": np.ascontiguousarray(np.asarray(L1_gnn_beta).reshape(NP, P, T).transpose(1, 0, 2)).reshape(P, NP * T),
    }
    nc = bacc.Bacc("TRN2", target_bir_lowering=False, num_devices=1)
    f32 = mybir.dt.float32
    aps = [nc.dram_tensor(k, v.shape, f32, kind="ExternalInput").ap() for k, v in arrays.items()]
    out = nc.dram_tensor("out", (N, F), f32, kind="ExternalOutput").ap()
    two_gnn_layers(nc, *aps, out)
    r = run_bass_kernel_spmd(nc, [arrays], core_ids=[0])
    return r.results[0]["out"]
```

```python
from contextlib import ExitStack

import concourse.bass as bass
from concourse import mybir

N = 4096
F = 128
P = 128
NP = 8
LAST = NP - 1
B = N // NP
T = B // P
HALF = T // 2 * B
SLOTS = 12
STAGING_SLOTS = 4
RESULT_SLOTS = 3
KEEP = [4] * 5 + [3, 3, 2]
SAVE_AT, SCALE_AT = 1, 2
RESIDUAL_AT = 4
STATS_STEP = 2
PIECES = T + T // STATS_STEP + 1
SELF_AT = 6
BIAS_AT = 14
NORMALISE0_AT = (0, 6, 11)
NORMALISE_AT = 13
PROJECT_AT = 0
BEHIND = 2
BETWEEN = [0, 1, 0, 1, 1, 1, 1]
EARLY = 2
AHEAD = 2
SPLIT = {(LAST, I) for I in range(NP)} | {(LAST - 1, I) for I in range(1, NP, 2)}
SPLIT_Y = sorted({J for J, I in SPLIT})
NHI, NLO = 4, 4
EPS = 1e-5
TINY = 1.2e-38
FINAL = [I for I in range(LAST) if LAST - I <= KEEP[LAST]] + [I for I in range(LAST) if LAST - I > KEEP[LAST]]
STORES = 2
SPARE = 4


class Use:

    def __init__(self, J, I):
        self.J, self.I, self.native = J, I, (J, I) not in SPLIT


class Load:

    def __init__(self, J, I, degree_pos):
        self.J, self.I, self.degree_pos = J, I, degree_pos
        self.waits = {}


def layer0_uses():
    stages = []
    for t in range(LAST):
        first = list(range(min(2, t - 1))) if t > 1 else []
        late = [t - 2, t - 1] if t == LAST - 1 else []
        rest = [J for J in range(t) if J not in first + late]
        stages.append([Use(J, t) for J in first] + [Use(t - 1, I) for I in range(t - 1, -1, -1)] + [Use(J, t) for J in rest])
    t = LAST
    stages.append([Use(J, t - 1) for J in late] + [Use(t - 1, I) for I in range(t - 1, -1, -1)])
    natives = [LAST - 2, LAST - 1] + list(range(LAST - 2))
    behind = [Use(J, t) for J in natives[:BEHIND]]
    natives = natives[BEHIND:]
    ending = []
    for n, I in enumerate(FINAL):
        ending.append(Use(t, I))
        ending += [Use(J, t) for J in natives[:BETWEEN[n]]]
        natives = natives[BETWEEN[n]:]
    ending.append(Use(t, t))
    assert not natives
    return stages, behind, ending


def layer0_loads():
    stages = []
    for t in range(NP):
        loads = [Load(J, t, J) for J in range(t)]
        again = [Load(t - 1, I, None) for I in range(t - 1, -1, -1) if t - 1 - I > KEEP[t - 1]]
        loads = loads[:2] + again + loads[2:]
        loads += [Load(J, t, J) for J in range(t, NP)]
        stages.append(loads)
    again = [Load(LAST, I, None) for I in FINAL if LAST - I > KEEP[LAST]]
    return stages, again


def degree_count(t, pos):
    return (NP - 1) * t + max(pos, 1)


def place_blocks():
    stages, behind, ending = layer0_uses()
    load_stages, again = layer0_loads()
    uses = [u for stage in stages for u in stage] + behind + ending
    loads = [l for st in load_stages for l in st] + again
    native = split = 0
    for n, u in enumerate(uses):
        u.position = n
        if u.native:
            u.index, native = native, native + 1
        else:
            u.index, split = split, split + 1
    reuse = [Use(J, LAST) for J in FINAL + [LAST]]
    for n, u in enumerate(reuse):
        u.native, u.index, u.position = False, split + n, len(uses) + n
    next_panel = [Load(J, LAST - 1, None) for J in range(NP)] + [Load(J, LAST - 2, None) for J in range(SPARE)]
    position_of = {(u.J, u.I): u.position for u in uses + reuse}
    staging_from = next(u.position for u in uses + reuse if not u.native) - AHEAD
    results_from = ending[0].position
    until = {}
    for n in range(SLOTS + STAGING_SLOTS + RESULT_SLOTS):
        until[n] = len(uses) + NP + 1 if n < SLOTS else staging_from if n < SLOTS + STAGING_SLOTS else results_from
    free = [(s, {}) for s in sorted(until, reverse=True)]
    held, dropped, queue = {}, [], uses + reuse
    taken = {n: 0 for n in until}
    position = 0
    staging_waits = {"native": 0, "degrees": 0}
    for n, l in enumerate(loads + next_panel):
        drops = l.degree_pos is not None and l.J - l.I > KEEP[l.J]
        last_use = next((u.position for u in stages[l.I + 1]), 0) if drops else position_of[(l.J, l.I)]
        if n >= len(loads):
            last_use = len(uses) + NP
        while True:
            fits = [f for f in free if last_use < until[f[0]]]
            if fits:
                break
            if dropped and dropped[0].degree_pos >= 1:
                d = dropped.pop(0)
                free.append((d.slot, {"degrees": degree_count(d.I, d.degree_pos)}))
                continue
            u = queue[position]
            b = held[(u.J, u.I)]
            u.load = b
            position += 1
            if u.I == LAST and u in uses:
                continue
            waits = {"native": u.index + 1} if u.native else {"split": 2 * u.index + 2}
            if u in reuse:
                waits |= {"native": before.index + 1 for before in uses if before.native and (before.J, before.I) == (u.J, u.I)}
            if b.degree_pos is not None:
                waits["degrees"] = degree_count(b.I, b.degree_pos)
            free.append((b.slot, waits))
            del held[(u.J, u.I)]
        free.remove(fits[0])
        l.slot, l.waits = fits[0]
        l.number, l.position = n, position
        taken[l.slot] += 1
        l.arrived = 16 * taken[l.slot]
        if SLOTS <= l.slot < SLOTS + STAGING_SLOTS and l.degree_pos is not None:
            staging_waits["degrees"] = max(staging_waits["degrees"], degree_count(l.I, l.degree_pos))
        if drops:
            dropped.append(l)
        else:
            held[(l.J, l.I)] = l
    for u in queue[position:]:
        u.load = held[(u.J, u.I)]
    staging_waits["native"] = sum(u.native for u in uses[:staging_from])
    return stages, behind, ending, load_stages, again, reuse, next_panel, split, staging_waits


def two_gnn_layers(nc, x, adj, w0t, b0, w1, b1, beta, out):
    f32, f32r = mybir.dt.float32, mybir.dt.float32r
    ALU, ACT = mybir.AluOpType, mybir.ActivationFunctionType
    stages, behind, ending, load_stages, again, reuse, next_panel, splits0, staging_waits = place_blocks()
    odd = {l.J: l for l in next_panel if l.I == LAST - 1}
    even = odd | {l.J: l for l in next_panel if l.I == LAST - 2}

    ctx = ExitStack()
    with ctx:
        def sb(name, shape, dt=f32):
            return ctx.enter_context(nc.sbuf_tensor(name, shape, dt))

        def sem(name):
            return ctx.enter_context(nc.semaphore(name))

        blocks = sb("blocks", [P, SLOTS, T * B])
        feat = sb("feat", [P, NP, T * F])
        others = [J for J in range(NP) if J not in SPLIT_Y]
        hi_y, lo_y = (sb(n, [P, len(SPLIT_Y), T * F], f32r) for n in ("hi_y", "lo_y"))
        with nc.sbuf_tensor("result_slots", [P, RESULT_SLOTS, T * B], f32) as result_slots:
            pass
        hi_x, lo_x = (sb(n, [P, len(others), T * F], f32r) for n in ("hi_x", "lo_x"))
        scaled = sb("scaled", [P, LAST, T * F])
        with nc.sbuf_tensor("staging_slots", [P, STAGING_SLOTS, T * B], f32) as staging_slots:
            pass
        hi_a = sb("hi_a", [P, NHI, HALF], f32r)
        lo_a = sb("lo_a", [P, NLO, HALF], f32r)
        work = sb("work", [P, T * B])
        part = work[:, :]
        z = work[:, 0:2 * B].rearrange("p (s c) -> p s c", s=2)
        agg = work[:, 2 * B:4 * B].rearrange("p (s c) -> p s c", s=2)
        w0_sb, w1_sb = sb("w0_sb", [F, F]), sb("w1_sb", [F, F])
        b0_sb, b1_sb = sb("b0_sb", [P, T * F]), sb("b1_sb", [P, T * F])
        ident, ident_r = sb("ident", [P, P]), sb("ident_r", [P, P], f32r)
        self_f = sb("self_f", [P, T * F])
        fold_f = self_f[:, :]
        biased = b0_sb
        ones = sb("ones", [P, 1])
        neg_half = sb("neg_half", [P, T])
        beta_sb, rowsum = sb("beta_sb", [P, NP * T]), sb("rowsum", [P, NP * T])
        dinv = sb("dinv", [P, NP * T])
        scale = sb("scale", [P, NP * T])
        positive, clamped, power = sb("positive", [P, T]), sb("clamped", [P, T]), sb("power", [P, T])
        scale4, beta4 = sb("scale4", [P, T]), sb("beta4", [P, T])
        stats, meanvar = sb("stats", [P, T, 6]), sb("meanvar", [P, T, 2])
        eps, zeros = sb("eps", [P, T]), sb("zeros", [P, T])
        vareps, rstd = sb("vareps", [P, T]), sb("rstd", [P, T])
        negmean, shift = sb("negmean", [P, T]), sb("shift", [P, T])

        bank = [ctx.enter_context(nc.psum_tensor(f"bank{i}", [P, B], f32)) for i in range(NP)]

        block_in = [sem(f"block_in{s}") for s in range(SLOTS + STAGING_SLOTS + RESULT_SLOTS)]
        x_in = [sem(f"x_in{t}") for t in range(NP)]
        consts_in = sem("consts_in")
        ident_zero, consts_set, ident_done, ident_r_done = (sem(n) for n in ("ident_zero", "consts_set", "ident_done", "ident_r_done"))
        degrees = sem("degrees")
        diagonal_ready = sem("diagonal_ready")
        folded = sem("folded")
        rowsum_ready = sem("rowsum_ready")
        rowsum_saved = sem("rowsum_saved")
        pool_step, vec_step, act_step = sem("pool_step"), sem("vec_step"), sem("act_step")
        dinv_ready = sem("dinv_ready")
        y_ready = sem("y_ready")
        hi_ready, lo_ready = sem("hi_ready"), sem("lo_ready")
        half_used = sem("half_used")
        native_used = sem("native_used")
        agg_ready = sem("agg_ready")
        proj_ready, proj_read = sem("proj_ready"), sem("proj_read")
        stats_ready = sem("stats_ready")
        var_ready, rstd_ready = sem("var_ready"), sem("rstd_ready")
        normed = sem("normed")
        hi_x_ready = sem("hi_x_ready")
        x1_ready = sem("x1_ready")
        self_ready = sem("self_ready")
        biased_ready = sem("biased_ready")
        scale_set = sem("scale_set")
        stored = [sem(f"stored{i}") for i in range(STORES)]

        x_v = x.rearrange("(b p k) f -> b p (k f)", b=NP, p=P)
        out_v = out.rearrange("(b p k) f -> b p (k f)", b=NP, p=P)
        adj_flat = adj.rearrange("i j p c -> (i j p c)")
        x1_order = FINAL + [LAST]

        def slot_of(n):
            if n < SLOTS:
                return blocks[:, n, :]
            n -= SLOTS
            return staging_slots[:, n, :] if n < STAGING_SLOTS else result_slots[:, n - STAGING_SLOTS, :]

        def diagonal(slot):
            b = slot_of(slot)
            return bass.AP(b.tensor, b.offset, [b.ap[0], [B + P, T], [1, P]])

        def hi(J):
            return hi_y[:, SPLIT_Y.index(J), :] if J in SPLIT_Y else hi_x[:, others.index(J), :]

        def lo(J):
            return lo_y[:, SPLIT_Y.index(J), :] if J in SPLIT_Y else lo_x[:, others.index(J), :]

        def split_of(s, J):
            return splits0 + NP * s + J

        def columns(s):
            if isinstance(s, int):
                return slice(s * T, (s + 1) * T)
            return bass.ds(s * T, T)

        def arrival(s, parity, J):
            if isinstance(s, int) and s == 0:
                return reuse[J].load.slot, reuse[J].load.arrived
            if J >= SPARE:
                return odd[J].slot, odd[J].arrived + (s - 1) * 16
            load, first = (even[J], 2) if parity == 0 else (odd[J], 1)
            return load.slot, load.arrived + (s - first) * 8

        def accumulator(parity):
            return bank[x1_order[parity]]

        def projected(parity):
            return bank[x1_order[2 + parity]]

        whole = ident[:, :]
        ident_wide = bass.AP(whole.tensor, whole.offset, [whole.ap[0], [0, T], [1, P]])

        block = ctx.enter_context(nc.Block())

        @block.sync
        def _(sync):
            def load(l):
                if "degrees" in l.waits:
                    sync.wait_ge(degrees, l.waits["degrees"])
                if "native" in l.waits:
                    sync.wait_ge(native_used, l.waits["native"])
                if "split" in l.waits:
                    sync.wait_ge(lo_ready, l.waits["split"])
                sync.dma_start(slot_of(l.slot), adj[LAST - l.I, LAST - l.J, :, :]).then_inc(block_in[l.slot], 16)

            for t in range(NP):
                for n, l in enumerate(load_stages[t]):
                    load(l)
                    if n == NP - 3:
                        sync.dma_start(feat[:, LAST - t, :], x_v[LAST - t, :, :]).then_inc(x_in[t], 16)
            for l in again + next_panel:
                load(l)

            def load1(s, parity, J):
                slot = (odd[J] if parity or J >= SPARE else even[J]).slot
                start = (s * NP + (LAST - J)) * (P * T * B)
                if not isinstance(s, int):
                    start = sync.snap(start)
                source = adj_flat[bass.ds(start, P * T * B)].rearrange("(p c) -> p c", p=P)
                sync.wait_ge(lo_ready, 2 * split_of(s - (1 if J >= SPARE else 2), J) + 2)
                sync.dma_start(blocks[:, slot, :], source).then_inc(block_in[slot], 16)

            def step_loads(s, parity):
                for J in range(SPARE, NP):
                    load1(s, parity, J)
                if not isinstance(s, int) or s < LAST:
                    for J in range(SPARE):
                        load1(s + 1, 1 - parity, J)

            with sync.Fori(0, NP // 2 - 2) as r:
                step_loads(2 * r + 2, 0)
                step_loads(2 * r + 3, 1)
            step_loads(LAST - 1, 0)
            step_loads(LAST, 1)

        @block.gpsimd
        def _(pool):
            nc.gpsimd.memset(ident[:, :], 0.0).then_inc(ident_zero, 1)
            nc.gpsimd.memset(ones[:, :], 1.0).then_inc(consts_set, 1)
            nc.gpsimd.memset(neg_half[:, :], -0.5).then_inc(consts_set, 1)
            nc.gpsimd.memset(eps[:, :], EPS).then_inc(consts_set, 1)
            nc.gpsimd.memset(zeros[:, :], 0.0).then_inc(consts_set, 1)
            pool.wait_ge(ident_zero, 1)
            nc.gpsimd.affine_select(out=ident[:, :], in_=ident[:, :], compare_op=ALU.not_equal, fill=1.0,
                                    base=0, pattern=[[-1, P]], channel_multiplier=1).then_inc(ident_done, 1)
            pool.wait_ge(consts_set, 4)
            for t in range(NP):
                pool.wait_ge(rowsum_saved, t + 1)
                cols = columns(LAST - t)
                nc.gpsimd.tensor_scalar(clamped[:, :], rowsum[:, cols], 1.0, TINY, ALU.add, ALU.max).then_inc(pool_step, 1)
                nc.gpsimd.tensor_scalar(positive[:, :], rowsum[:, cols], 1.0, 0.0, ALU.add, ALU.is_gt).then_inc(pool_step, 1)
                pool.wait_ge(pool_step, 3 * t + 2)
                nc.gpsimd.tensor_tensor(power[:, :], clamped[:, :], neg_half[:, :], ALU.pow).then_inc(pool_step, 1)
                pool.wait_ge(pool_step, 3 * t + 3)
                nc.gpsimd.tensor_tensor(dinv[:, cols], power[:, :], positive[:, :], ALU.mult).then_inc(dinv_ready, 1)

            def deviation(e):
                steps = 3 * NP + 3 * e
                pool.wait_ge(var_ready, e + 1)
                nc.gpsimd.tensor_tensor(vareps[:, :], meanvar[:, :, 1], eps[:, :], ALU.add).then_inc(pool_step, 1)
                nc.gpsimd.tensor_tensor(negmean[:, :], zeros[:, :], meanvar[:, :, 0], ALU.subtract).then_inc(pool_step, 1)
                if not isinstance(e, int) or e >= 1:
                    pool.wait_ge(normed, e)
                pool.wait_ge(pool_step, steps + 2)
                nc.gpsimd.tensor_tensor(rstd[:, :], vareps[:, :], neg_half[:, :], ALU.pow).then_inc(pool_step, 1)
                pool.wait_ge(pool_step, steps + 3)
                nc.gpsimd.tensor_tensor(shift[:, :], negmean[:, :], rstd[:, :], ALU.mult).then_inc(rstd_ready, 1)

            deviation(0)
            with pool.Fori(1, 2 * NP) as e:
                deviation(e)

        @block.scalar
        def _(act):
            for dst, src in ((w0_sb, w0t), (w1_sb, w1), (b0_sb, b0), (b1_sb, b1), (beta_sb, beta)):
                act.dma_start(dst[:, :], src).then_inc(consts_in, 16)
            act.wait_ge(ident_done, 1)
            nc.scalar.activation(ident_r[:, :], ident[:, :], ACT.Copy).then_inc(ident_r_done, 1)

            def hi_half(q, h, slot, count):
                if h == 0:
                    act.wait_ge(block_in[slot], count)
                if not isinstance(q, int) or 2 * q + h >= NHI:
                    act.wait_ge(half_used, 2 * q + h - (NHI - 1))
                buf = (2 * hi_half.static + h) % NHI
                nc.scalar.activation(hi_a[:, buf, :], slot_of(slot)[:, h * HALF:(h + 1) * HALF], ACT.Copy).then_inc(hi_ready, 1)

            def hi_use(u):
                hi_half.static = u.index
                if u.J == u.I and u.I != LAST:
                    act.wait_ge(diagonal_ready, u.I + 1)
                for h in range(2):
                    hi_half(u.index, h, u.load.slot, u.load.arrived)

            def copy_out(e, bank_of, buf):
                if not isinstance(e, int) or e >= 2:
                    act.wait_ge(proj_ready, e - 1)
                else:
                    act.wait_ge(dinv_ready, NP)
                nc.scalar.activation(agg[:, buf, :], bank_of[:, :], ACT.Copy).then_inc(agg_ready, 1)

            def normalise(e, dst, buf, tiles=range(T)):
                if tiles[0] == 0:
                    act.wait_ge(rstd_ready, e + 1)
                for k in tiles:
                    last = nc.scalar.activation(dst[:, k * F:(k + 1) * F], z[:, buf, k * F:(k + 1) * F], ACT.Identity,
                                                bias=shift[:, k:k + 1], scale=rstd[:, k:k + 1])
                if tiles[-1] == T - 1:
                    last.then_inc(normed, 1)

            def normalise0(e):
                I = x1_order[e]
                normalise(e, feat[:, LAST - I, :], e % 2)
                act.wait_ge(normed, e + 1)
                nc.scalar.activation(hi(I), feat[:, LAST - I, :], ACT.Copy).then_inc(hi_x_ready, 1)

            act.wait_ge(native_used, staging_waits["native"])
            act.wait_ge(degrees, staging_waits["degrees"])
            row = [u for u in ending if u.J == LAST]
            for u in [u for stage in stages for u in stage] + behind:
                if not u.native:
                    hi_use(u)
            for n, u in enumerate(row):
                hi_use(u)
                if n >= 3:
                    normalise0(n - 3)
                if n >= 1:
                    act.wait_ge(half_used, 2 * row[n - 1].index + 2)
                    copy_out(n - 1, bank[row[n - 1].I], (n - 1) % 2)

            def layer1_step(s, parity, first=False):
                for J in range(NP):
                    slot, count = arrival(s, parity, J)
                    q = split_of(s, J)
                    hi_half.static = splits0 + J
                    for h in range(2):
                        hi_half(q, h, slot, count)
                        piece = 2 * J + h
                        if piece == 2:
                            act.wait_ge(half_used, 2 * split_of(s, 0))
                            copy_out(s + NP - 1, bank[LAST] if first else accumulator(1 - parity), 1 - parity)
                        if first and piece in NORMALISE0_AT:
                            normalise0(NP - 3 + NORMALISE0_AT.index(piece))
                        if first and piece == NORMALISE0_AT[2] + 1:
                            for k in range(T):
                                self_term(s, k)
                        if not first and 0 <= piece - SELF_AT < T:
                            self_term(s, piece - SELF_AT)
                        if not first and 0 <= 2 * (piece - NORMALISE_AT) < T:
                            tile = 2 * (piece - NORMALISE_AT)
                            normalise(s - 1 + NP, z[:, 1 - parity, :], 1 - parity, range(tile, tile + 2))
                if not first:
                    store(s - 1, 1 - parity)

            def self_term(s, k):
                if k == 0:
                    nc.scalar.activation(beta4[:, :], beta_sb[:, columns(s)], ACT.Copy).then_inc(act_step, 1)
                    act.wait_ge(act_step, s + 1)
                last = nc.scalar.activation(self_f[:, k * F:(k + 1) * F], feat[:, s, k * F:(k + 1) * F],
                                            ACT.Copy, scale=beta4[:, k:k + 1])
                if k == T - 1:
                    last.then_inc(self_ready, 1)

            def store(s, buf):
                act.wait_ge(normed, s + NP + 1)
                act.dma_start(out_v[s, :, :], z[:, buf, :]).then_inc(stored[buf], 16)

            act.wait_ge(consts_in, 80)
            layer1_step(0, 0, first=True)
            layer1_step(1, 1)
            with act.Fori(0, NP // 2 - 1) as r:
                layer1_step(2 * r + 2, 0)
                layer1_step(2 * r + 3, 1)
            act.wait_ge(half_used, 2 * split_of(NP, 0))
            copy_out(2 * NP - 1, accumulator(1), 1)
            normalise(2 * NP - 1, z[:, 1, :], 1)
            store(LAST, 1)
            act.wait_ge(stored[0], 16 * (NP // 2))
            act.wait_ge(stored[1], 16 * (NP // 2))

        @block.vector
        def _(vec):
            steps = [0]

            def link(instruction):
                instruction.then_inc(vec_step, 1)
                steps[0] += 1
                vec.wait_ge(vec_step, steps[0])

            def degree(l):
                if l.degree_pos == 0:
                    return
                vec.wait_ge(block_in[l.slot], l.arrived)
                if l.degree_pos == 1:
                    if l.I >= 1:
                        vec.wait_ge(folded, l.I)
                    other = load_stages[l.I][0]
                    vec.wait_ge(block_in[other.slot], other.arrived)
                    first = slot_of(other.slot)
                else:
                    vec.wait_ge(degrees, degree_count(l.I, l.degree_pos) - 1)
                    first = part
                nc.vector.tensor_tensor(part, first, slot_of(l.slot), ALU.add).then_inc(degrees, 1)
                if l.degree_pos == max(l.I, 1) and l.I != LAST:
                    own = diagonal(other.slot if l.I == 0 else l.slot)
                    vec.wait_ge(degrees, degree_count(l.I, l.degree_pos))
                    vec.wait_ge(ident_done, 1)
                    nc.vector.tensor_tensor(own, own, ident_wide, ALU.add).then_inc(diagonal_ready, 1)

            def lo_half(q, h, slot, static):
                vec.wait_ge(hi_ready, 2 * q + h + 1)
                if not isinstance(q, int) or 2 * q + h >= NLO:
                    vec.wait_ge(half_used, 2 * q + h - (NLO - 1))
                hi_part = hi_a[:, (2 * static + h) % NHI, :].bitcast(f32)
                nc.vector.tensor_tensor(lo_a[:, (2 * static + h) % NLO, :], slot_of(slot)[:, h * HALF:(h + 1) * HALF],
                                        hi_part, ALU.subtract).then_inc(lo_ready, 1)

            def lo_use(u):
                for h in range(2):
                    lo_half(u.index, h, u.load.slot, u.index)

            def fold(t):
                vec.wait_ge(degrees, degree_count(t, NP - 1))
                link(nc.vector.tensor_tensor(part[:, 0:2 * B], part[:, 0:2 * B], part[:, 2 * B:4 * B], ALU.add))
                nc.vector.tensor_tensor(fold_f[:, :], part[:, 0:B], part[:, B:2 * B], ALU.add).then_inc(folded, 1)

            def save_rowsum(t):
                vec.wait_ge(rowsum_ready, t + 1)
                nc.vector.tensor_copy(rowsum[:, columns(LAST - t)], bank[LAST][:, 0:T]).then_inc(rowsum_saved, 1)

            def scale_features(t):
                vec.wait_ge(x_in[t], 16)
                vec.wait_ge(dinv_ready, t + 1)
                y = scaled[:, t, :] if t < LAST else fold_f[:, :]
                for k in range(T):
                    last = nc.vector.tensor_scalar(y[:, k * F:(k + 1) * F], feat[:, LAST - t, k * F:(k + 1) * F],
                                                   dinv[:, columns(LAST - t)][:, k:k + 1], None, ALU.mult)
                if t not in SPLIT_Y:
                    last.then_inc(y_ready, 1)
                else:
                    link(last)
                    link(nc.vector.tensor_copy(hi(t), y))
                    nc.vector.tensor_tensor(lo(t), y, hi(t).bitcast(f32), ALU.subtract).then_inc(y_ready, 1)
                if t == 0:
                    vec.wait_ge(consts_in, 80)
                vec.wait_ge(y_ready, t + 1)
                link(nc.vector.tensor_tensor(feat[:, LAST - t, :], feat[:, LAST - t, :], b0_sb[:, :], ALU.add))

            def residual(e, proj_bank, features, factor, buf, tiles=range(T)):
                if tiles[0] == 0:
                    if not isinstance(e, int) or e >= 2:
                        vec.wait_ge(normed, e - 1)
                    vec.wait_ge(proj_ready, e + 1)
                for k in tiles:
                    last = nc.vector.scalar_tensor_tensor(z[:, buf, k * F:(k + 1) * F], proj_bank[:, k * F:(k + 1) * F],
                                                          factor[:, k:k + 1], features[:, k * F:(k + 1) * F],
                                                          ALU.mult, ALU.add)
                if tiles[-1] == T - 1:
                    last.then_inc(proj_read, 1)

            def row_stats(e, buf, tiles=range(T)):
                if tiles[0] == 0:
                    vec.wait_ge(proj_read, e + 1)
                for k in tiles:
                    last = nc.vector.bn_stats(stats[:, k, :], z[:, buf, k * F:(k + 1) * F])
                if tiles[-1] == T - 1:
                    last.then_inc(stats_ready, 1)

            def moments(e, next_scale=None):
                vec.wait_ge(stats_ready, e + 1)
                if not isinstance(e, int) or e >= 1:
                    vec.wait_ge(rstd_ready, e)
                if next_scale is not None:
                    nc.vector.tensor_copy(scale4[:, :], scale[:, columns(next_scale)]).then_inc(scale_set, 1)
                for k in range(T):
                    last = nc.vector.bn_aggr(meanvar[:, k, :], stats[:, k, :])
                last.then_inc(var_ready, 1)

            def residual0(e):
                I = x1_order[e]
                residual(e, bank[I], feat[:, LAST - I, :], dinv[:, columns(LAST - I)], e % 2)

            def split0(e):
                I = x1_order[e]
                vec.wait_ge(hi_x_ready, e + 1)
                nc.vector.tensor_tensor(lo(I), feat[:, LAST - I, :], hi(I).bitcast(f32), ALU.subtract).then_inc(x1_ready, 1)

            vec.wait_ge(consts_set, 1)
            for t in range(NP):
                pending = [u for u in stages[t] if not u.native]
                chain = [(SAVE_AT, save_rowsum), (SCALE_AT, scale_features)] if t >= 1 else []
                needs_y = [u.position for u in stages[t] if u.J == t - 1][:1]
                for n, l in enumerate(load_stages[t]):
                    while chain and (n >= chain[0][0] or l.position > needs_y[0]):
                        chain.pop(0)[1](t - 1)
                    while pending and pending[0].position < l.position:
                        lo_use(pending.pop(0))
                    if l.degree_pos is not None:
                        degree(l)
                        if pending and not chain and pending[0].load.number <= l.number:
                            lo_use(pending.pop(0))
                fold(t)
                for u in pending:
                    lo_use(u)
            save_rowsum(LAST)
            early = [u for u in behind + ending if not u.native][:EARLY]
            for u in early:
                lo_use(u)
            scale_features(LAST)
            link(nc.vector.tensor_tensor(scale[:, :], rowsum[:, :], beta_sb[:, :], ALU.add))
            link(nc.vector.reciprocal(scale[:, :], scale[:, :]))
            nc.vector.tensor_copy(scale4[:, :], scale[:, columns(0)]).then_inc(scale_set, 1)
            for n, u in enumerate(u for u in ending if u.J == LAST):
                if u not in early:
                    lo_use(u)
                if n >= 4:
                    split0(n - 4)
                if n >= 2:
                    residual0(n - 2)
                    row_stats(n - 2, n % 2)
                    moments(n - 2)

            def layer1_step(s, parity, first=False):
                for J in range(NP):
                    slot = arrival(s, parity, J)[0]
                    for h in range(2):
                        lo_half(split_of(s, J), h, slot, splits0 + J)
                        done = 2 * J + h
                        if first:
                            last_epilogues(done)
                        elif 0 <= done - RESIDUAL_AT < PIECES:
                            epilogue(s - 1, 1 - parity, done - RESIDUAL_AT)
                        if done == (2 * NP - 1 if first else BIAS_AT):
                            vec.wait_ge(x1_ready, NP)
                            vec.wait_ge(proj_read, s + NP)
                            nc.vector.tensor_tensor(biased[:, :], feat[:, s, :], b1_sb[:, :], ALU.add).then_inc(biased_ready, 1)

            def last_epilogues(done):
                for e, at in ((NP - 2, 1), (LAST, 5)):
                    if done == at:
                        residual0(e)
                    if done == at + 1:
                        row_stats(e, e % 2)
                    if done == at + 2:
                        moments(e)
                for e, at in ((NP - 4, 0), (NP - 3, 4), (NP - 2, 9), (LAST, 13)):
                    if done == at:
                        split0(e)

            def epilogue(s, buf, piece):
                if piece == 0:
                    vec.wait_ge(scale_set, s + 1)
                    if not isinstance(s, int) or s >= STORES:
                        vec.wait_ge(stored[buf], store_count(s, buf))
                    vec.wait_ge(biased_ready, s + 1)
                if piece < T:
                    residual(s + NP, projected(buf), biased[:, :], scale4, buf, range(piece, piece + 1))
                elif piece < PIECES - 1:
                    tile = STATS_STEP * (piece - T)
                    row_stats(s + NP, buf, range(tile, tile + STATS_STEP))
                else:
                    moments(s + NP, None if isinstance(s, int) and s == LAST else s + 1)

            def store_count(s, buf):
                return (s - buf) * 8

            layer1_step(0, 0, first=True)
            layer1_step(1, 1)
            with vec.Fori(0, NP // 2 - 1) as r:
                layer1_step(2 * r + 2, 0)
                layer1_step(2 * r + 3, 1)
            for piece in range(PIECES):
                epilogue(LAST, 1, piece)

        @block.tensor
        def _(pe):
            opened = set()

            def opens(b):
                if b in opened:
                    return False
                opened.add(b)
                return True

            def block_native(u, stop):
                pe.wait_ge(y_ready, u.J + 1)
                pe.wait_ge(block_in[u.load.slot], u.load.arrived)
                for k in range(T):
                    last = nc.tensor.matmul(bank[u.I][:, :], scaled[:, u.J, k * F:(k + 1) * F],
                                            slot_of(u.load.slot)[:, k * B:(k + 1) * B], start=opens(u.I),
                                            stop=stop and k == T - 1)
                last.then_inc(native_used, 1)

            def block_split(J, q, static, dst, start, stop):
                for h in range(2):
                    pe.wait_ge(lo_ready, 2 * q + h + 1)
                    for k in range(T // 2):
                        tile = (h * (T // 2) + k) * F
                        hf, lf = hi(J)[:, tile:tile + F], lo(J)[:, tile:tile + F]
                        ha = hi_a[:, (2 * static + h) % NHI, k * B:(k + 1) * B]
                        la = lo_a[:, (2 * static + h) % NLO, k * B:(k + 1) * B]
                        done = stop and h == 1 and k == T // 2 - 1
                        nc.tensor.matmul(dst[:, :], hf, ha, start=start and h == 0 and k == 0, stop=False)
                        nc.tensor.matmul(dst[:, :], hf, la, start=False, stop=False)
                        last = nc.tensor.matmul(dst[:, :], lf, ha, start=False, stop=done)
                    last.then_inc(half_used, 1)

            def add_self(t):
                pe.wait_ge(ident_r_done, 1)
                for k in range(T):
                    for f in (hi(t), lo(t)):
                        nc.tensor.matmul(bank[t][:, k * P:(k + 1) * P], f[:, k * F:(k + 1) * F], ident_r[:, :],
                                         start=False, stop=False)

            def layer0_block(u, stop=False):
                pe.wait_ge(y_ready, u.J + 1)
                if u.J == u.I and u.I != LAST:
                    pe.wait_ge(diagonal_ready, u.I + 1)
                if u.native:
                    block_native(u, stop)
                else:
                    block_split(u.J, u.index, u.index, bank[u.I], opens(u.I), stop)

            def sum_degrees(t):
                pe.wait_ge(folded, t + 1)
                if t >= 1:
                    pe.wait_ge(rowsum_saved, t)
                for g in range(T):
                    last = nc.tensor.matmul(bank[LAST][:, g:g + 1], fold_f[:, g * P:(g + 1) * P], ones[:, :],
                                            start=True, stop=True)
                last.then_inc(rowsum_ready, 1)

            def project(e, dst, weights, buf):
                pe.wait_ge(agg_ready, e + 1)
                for k in range(T):
                    last = nc.tensor.matmul(dst[:, k * F:(k + 1) * F], agg[:, buf, k * P:(k + 1) * P],
                                            weights[:, :], start=True, stop=True)
                last.then_inc(proj_ready, 1)

            def project0(e):
                project(e, bank[x1_order[e]], w0_sb, e % 2)

            pe.wait_ge(consts_set, 1)
            pe.wait_ge(consts_in, 80)
            for t, stage in enumerate(stages):
                for u in stage:
                    layer0_block(u)
                sum_degrees(t)
            pe.wait_ge(rowsum_saved, NP)
            for u in behind:
                layer0_block(u)
            completed = []
            for u in ending:
                if u.J == u.I:
                    add_self(LAST)
                layer0_block(u, stop=u.J == LAST)
                if completed:
                    project0(x1_order.index(completed.pop()))
                if u.J == LAST and u.I != LAST:
                    completed.append(u.I)

            def layer1_step(s, parity, first=False):
                acc = accumulator(parity)
                for J in range(NP):
                    if first:
                        pe.wait_ge(x1_ready, J + 1)
                    if J == LAST:
                        pe.wait_ge(self_ready, s + 1)
                        for k in range(T):
                            nc.tensor.matmul(acc[:, k * P:(k + 1) * P], self_f[:, k * F:(k + 1) * F], ident[:, :],
                                             start=False, stop=False)
                    block_split(x1_order[J] if first else J, split_of(s, J), splits0 + J, acc, J == 0, J == LAST)
                    if J == (1 if first else PROJECT_AT):
                        if first:
                            project0(LAST)
                        else:
                            if not isinstance(s, int) or s >= 3:
                                pe.wait_ge(proj_read, s + NP - 2)
                            project(s + NP - 1, projected(1 - parity), w1_sb, 1 - parity)

            pe.wait_ge(proj_read, 4)
            layer1_step(0, 0, first=True)
            layer1_step(1, 1)
            with pe.Fori(0, NP // 2 - 1) as r:
                layer1_step(2 * r + 2, 0)
                layer1_step(2 * r + 3, 1)
            project(2 * NP - 1, projected(1), w1_sb, 1)


def kernel(x, adj, L0_gnn_W, L0_gnn_b, L1_gnn_kernel, L1_gnn_bias, L1_gnn_beta):
    import numpy as np
    import concourse.bacc as bacc
    from concourse.bass_utils import run_bass_kernel_spmd

    a = np.asarray(adj).reshape(NP, P, T, NP, P, T)
    arrays = {
        "x_in": np.ascontiguousarray(x),
        "adj_in": np.ascontiguousarray(a.transpose(0, 3, 4, 5, 2, 1)).reshape(NP, NP, P, T * B),
        "w0t_in": np.ascontiguousarray(np.asarray(L0_gnn_W).T),
        "b0_in": np.ascontiguousarray(np.tile(np.asarray(L0_gnn_b), (P, T))),
        "w1_in": np.ascontiguousarray(L1_gnn_kernel),
        "b1_in": np.ascontiguousarray(np.tile(np.asarray(L1_gnn_bias), (P, T))),
        "beta_in": np.ascontiguousarray(np.asarray(L1_gnn_beta).reshape(NP, P, T).transpose(1, 0, 2)).reshape(P, NP * T),
    }
    nc = bacc.Bacc("TRN2", target_bir_lowering=False, num_devices=1)
    f32 = mybir.dt.float32
    aps = [nc.dram_tensor(k, v.shape, f32, kind="ExternalInput").ap() for k, v in arrays.items()]
    out = nc.dram_tensor("out", (N, F), f32, kind="ExternalOutput").ap()
    two_gnn_layers(nc, *aps, out)
    r = run_bass_kernel_spmd(nc, [arrays], core_ids=[0])
    return r.results[0]["out"]
```
